# Optimizing a Trainium2 kernel written in Bass

```python
import numpy as np
import jax
import jax.numpy as jnp

def _softmax(x, axis=-1):
    return jax.nn.softmax(x, axis=axis)

def _gelu(x):
    return jax.nn.gelu(x, approximate=True)

def _silu(x):
    return jax.nn.silu(x)

def _sigmoid(x):
    return jax.nn.sigmoid(x)

def _layernorm(x, axis=-1, eps=1e-05):
    m = jnp.mean(x, axis=axis, keepdims=True)
    v = jnp.var(x, axis=axis, keepdims=True)
    return (x - m) / jnp.sqrt(v + eps)

def _scatter_add(tgt, idx, src, axis=0):
    return tgt.at[idx].add(src)

def _segment_sum(src, seg, n):
    return jax.ops.segment_sum(src, seg, n)
kernel_name = 'mk_gnn_resnorm_d1_gnn_r64_f66c49'

def setup_inputs(seed: int=0):
    np.random.seed(seed)
    _w = jnp.asarray

    def _rec_inputs():
        import jax
        import jax.numpy as jnp
        _gk = jax.random.key(seed)
        x = -0.000202 + 1 * jax.random.normal(jax.random.fold_in(_gk, 1), (100000, 128), jnp.float32)
        src = jax.random.randint(jax.random.fold_in(_gk, 2), (25000,), 0, 100000, jnp.int32)
        dst = jax.random.randint(jax.random.fold_in(_gk, 3), (25000,), 0, 100000, jnp.int32)
        _o = jnp.argsort(dst, stable=True)
        src = src[_o]
        dst = dst[_o]
        return (x, src, dst)
    x, src, dst = _rec_inputs()

    def _L0_gnn_setup():
        import jax, jax.numpy as jnp
        import numpy as np
        N_NODES = 50000
        N_EDGES = 12500
        H = 128
        T = 2
        key = jax.random.key(seed)
        ks = jax.random.split(key, 8)
        s = 0.05
        return {'h': jax.random.normal(ks[0], (N_NODES, H), jnp.float32), 'edges': jax.random.randint(ks[1], (N_EDGES, 2), 0, N_NODES, jnp.int64), 'W_msg': jax.random.normal(ks[2], (T, 2 * H, 2 * H), jnp.float32) * s, 'b_msg': jax.random.normal(ks[3], (T, 2 * H), jnp.float32) * s, 'W_ih': jax.random.normal(ks[4], (T, 3 * H, 2 * H), jnp.float32) * s, 'W_hh': jax.random.normal(ks[5], (T, 3 * H, H), jnp.float32) * s, 'b_ih': jax.random.normal(ks[6], (T, 3 * H), jnp.float32) * s, 'b_hh': jax.random.normal(ks[7], (T, 3 * H), jnp.float32) * s}
    _L0_gnn_all = _L0_gnn_setup()
    _L0_gnn_in = {k: v for k, v in _L0_gnn_all.items() if k in ('W_msg', 'b_msg', 'W_ih', 'W_hh', 'b_ih', 'b_hh')}
    del _L0_gnn_all
    return {'x': x, 'src': src, 'dst': dst, 'L0_gnn_W_msg': _L0_gnn_in['W_msg'], 'L0_gnn_b_msg': _L0_gnn_in['b_msg'], 'L0_gnn_W_ih': _L0_gnn_in['W_ih'], 'L0_gnn_W_hh': _L0_gnn_in['W_hh'], 'L0_gnn_b_ih': _L0_gnn_in['b_ih'], 'L0_gnn_b_hh': _L0_gnn_in['b_hh']}

def reference(x, src, dst, L0_gnn_W_msg, L0_gnn_b_msg, L0_gnn_W_ih, L0_gnn_W_hh, L0_gnn_b_ih, L0_gnn_b_hh):
    import jax
    import jax.numpy as jnp

    def _L0_gnn_ref(h, edges, W_msg, b_msg, W_ih, W_hh, b_ih, b_hh):
        import jax, jax.numpy as jnp
        import numpy as np
        N_NODES = 50000
        N_EDGES = 12500
        H = 128
        T = 2
        n_nodes, hd = h.shape
        src, dst = (edges[:, 0], edges[:, 1])
        deg = jax.ops.segment_sum(jnp.ones(edges.shape[0], h.dtype), dst, num_segments=n_nodes)
        has_msg = (deg > 0)[:, None]
        for t in range(W_msg.shape[0]):
            m_in = jnp.concatenate([h[src], h[dst]], axis=-1)
            m = m_in @ W_msg[t].T + b_msg[t]
            agg = jax.ops.segment_sum(m, dst, num_segments=n_nodes)
            gi = agg @ W_ih[t].T + b_ih[t]
            gh = h @ W_hh[t].T + b_hh[t]
            ir, iz, inn = (gi[:, :hd], gi[:, hd:2 * hd], gi[:, 2 * hd:])
            hr, hz, hn = (gh[:, :hd], gh[:, hd:2 * hd], gh[:, 2 * hd:])
            r = jax.nn.sigmoid(ir + hr)
            z = jax.nn.sigmoid(iz + hz)
            n = jnp.tanh(inn + r * hn)
            h_new = (1.0 - z) * n + z * h
            h = jnp.where(has_msg, h_new, h)
        return h
    edge_index_t = jnp.stack([src, dst], axis=1)
    x = _layernorm(x + _L0_gnn_ref(x, edge_index_t, L0_gnn_W_msg, L0_gnn_b_msg, L0_gnn_W_ih, L0_gnn_W_hh, L0_gnn_b_ih, L0_gnn_b_hh), axis=-1)
    return x

_drawn_inputs = setup_inputs


def setup_inputs(seed=0):
    import zlib

    import numpy as np

    out = dict(_drawn_inputs(seed))
    spreads = {}
    factors = {'L0_gnn_b_msg': 6.613, 'L0_gnn_b_ih': 5.745, 'L0_gnn_b_hh': 8.0}
    for name, (base, spread) in spreads.items():
        noise = np.random.default_rng([zlib.crc32(name.encode()), seed]).standard_normal(out[name].shape)
        drawn = base * np.exp(spread * noise) if base else spread * noise
        out[name] = jnp.asarray(drawn.astype(out[name].dtype))
    for name, factor in factors.items():
        out[name] = (out[name] * factor).astype(out[name].dtype)
    return out
```

```python
from contextlib import ExitStack

import concourse.bass as bass
from concourse import mybir

P = 128
TILES = 4
SLOTS = P * TILES
RING = 4
LAG = 3
LN_ROWS = 16
SKIP = float(1 << 20)
EPS = 1e-5

F32 = mybir.dt.float32
BF16 = mybir.dt.bfloat16
I32 = mybir.dt.int32
ALU = mybir.AluOpType
ACT = mybir.ActivationFunctionType


def build(nc, x, src, dst, W_msg, b_msg, W_ih, W_hh, b_ih, b_hh, out):
    N, H = x.shape
    E = src.shape[0]
    assert H == P and W_msg.shape[0] == 2
    NB = -(-E // SLOTS)
    NT = NB * TILES
    EP = NB * SLOTS
    BODIES = (NB - 1) // RING
    assert NB == BODIES * RING + 1 and BODIES >= 4
    LAST = NB - 1
    LN_FULL = N // (P * LN_ROWS)
    LN_TAIL_P = (N - LN_FULL * P * LN_ROWS) // LN_ROWS
    assert LN_TAIL_P * LN_ROWS + LN_FULL * P * LN_ROWS == N and 0 < LN_TAIL_P < P
    LN_1A = 2 * BODIES
    LN_BODIES = (LN_FULL - LN_1A) // 4
    assert LN_1A + 4 * LN_BODIES == LN_FULL and 2 * 4 * LN_BODIES + 1 == NB
    COPY = -(-N // (NB * 16)) * 16
    COPY_LAST = N - COPY * LAST
    assert 0 < COPY_LAST <= COPY
    GATES = 4 * P

    ctx = ExitStack()
    with ctx:
        def sb(name, shape, dt=F32):
            return ctx.enter_context(nc.sbuf_tensor(name, shape, dt))

        def sem(name):
            return ctx.enter_context(nc.semaphore(name))

        def sems(name, n):
            return [sem(f"{name}{k}") for k in range(n)]

        dst_s = nc.dram_tensor("dst_s", [EP + 2], I32, kind="Internal").ap()
        src_s = nc.dram_tensor("src_s", [EP], I32, kind="Internal").ap()
        h_table = nc.dram_tensor("h_table", [N, P], F32, kind="Internal").ap()
        xd_spill = nc.dram_tensor("xd_spill", [NB, P, SLOTS], F32, kind="Internal").ap()
        rows_spill = nc.dram_tensor("rows_spill", [3, EP], BF16, kind="Internal").ap()

        deg_spill = nc.dram_tensor("deg_spill", [1, EP], F32, kind="Internal").ap()

        h1 = sb("h1", [P, EP])
        srcbuf = [sb(f"srcbuf{k}", [P, SLOTS]) for k in range(RING)]
        dstbuf = [sb(f"dstbuf{k}", [P, SLOTS]) for k in range(RING)]
        lnbuf = [sb(f"lnbuf{k}", [P, LN_ROWS, P]) for k in range(4)]
        aT = [sb(f"aT{k}", [P, SLOTS]) for k in range(2)]
        dhT = [sb(f"dhT{k}", [P, SLOTS]) for k in range(2)]
        hT = [sb(f"hT{k}", [P, SLOTS]) for k in range(2)]
        rz = [sb(f"rz{k}", [P, 2, 2 * P]) for k in range(2)]
        npre = [sb(f"npre{k}", [P, 2, P]) for k in range(2)]
        nn = [sb(f"nn{k}", [P, 2, P]) for k in range(2)]
        dd = [sb(f"dd{k}", [P, 2, P]) for k in range(2)]
        hout = [sb(f"hout{k}", [P, 2, P]) for k in range(2)]
        window = [sb(f"window{k}", [P, SLOTS + 1], I32) for k in range(2)]
        same = [sb(f"same{k}", [P, SLOTS], BF16) for k in range(2)]
        degf = [sb(f"degf{k}", [64, SLOTS]) for k in range(2)]
        degl = [sb(f"degl{k}", [96, SLOTS], BF16) for k in range(2)]
        ones = sb("ones", [64, SLOTS], BF16)
        idx_all = sb("idx_all", [P, NB, 3, TILES], I32)
        stage = [sb(f"stage{k}", [P, 2 * TILES], I32) for k in range(RING)]
        stage_out = [sb(f"stage_out{k}", [P, TILES], I32) for k in range(RING)]
        WA = [sb(f"WA{t}", [P, 3 * P]) for t in range(2)]
        WD = [sb(f"WD{t}", [P, 3 * P]) for t in range(2)]
        WH = [sb(f"WH{t}", [P, 3 * P]) for t in range(2)]
        WB = [sb(f"WB{t}", [96, GATES], BF16) for t in range(2)]
        ident = sb("ident", [P, P])
        sel = sb("sel", [P, 3])
        eps_col = sb("eps_col", [P, 1])
        st = [sb(f"st{k}", [P, LN_ROWS, 6]) for k in range(2)]
        small = [sb(f"small{k}", [P, 8, LN_ROWS]) for k in range(2)]
        pad_idx = sb("pad_idx", [1, 2 * P], I32)

        psS = [ctx.enter_context(nc.psum_tensor(f"psS{k}", [P, SLOTS], F32)) for k in range(2)]
        psD = [ctx.enter_context(nc.psum_tensor(f"psD{k}", [P, SLOTS], F32)) for k in range(2)]
        psG = [ctx.enter_context(nc.psum_tensor(f"psG{k}", [P, 2, GATES], F32)) for k in range(2)]

        deg_rep = [w[:, 0:SLOTS].bitcast(F32) for w in window]

        off = [0]

        def over_h1(cols, dt=F32):
            a = h1[:, off[0]:off[0] + cols]
            off[0] += cols
            return a if dt is F32 else a.bitcast(dt)

        raw_idx = [over_h1(2 * P, I32) for _ in range(3)]
        f_idx = [over_h1(2 * P) for _ in range(3)]
        f_same = over_h1(2 * P)
        f_out = over_h1(2 * P)
        wmsg_sb = [over_h1(2 * 2 * P).rearrange("p (c f) -> p c f", c=2) for _ in range(2)]
        wih_sb = [over_h1(3 * 2 * P).rearrange("p (g f) -> p g f", g=3) for _ in range(2)]
        whh_sb = [over_h1(3 * P).rearrange("p (g f) -> p g f", g=3) for _ in range(2)]
        wihT = [over_h1(2 * 3 * P).rearrange("p (c g) -> p c g", c=2) for _ in range(2)]
        bm_col = [over_h1(2) for _ in range(2)]
        bm_rep = [over_h1(2 * 96).rearrange("p (c r) -> p c r", c=2) for _ in range(2)]
        bih_rep = [over_h1(3 * P) for _ in range(2)]
        bhh_rep = [over_h1(3 * P) for _ in range(2)]
        bias_f = [over_h1(GATES) for _ in range(2)]
        part = [[over_h1(GATES // 2, BF16) for _ in range(3)] for _ in range(2)]
        rest = [[over_h1(GATES) for _ in range(2)] for _ in range(2)]
        pick = [[over_h1(GATES) for _ in range(3)] for _ in range(2)]
        assert off[0] <= EP

        pad_set = sem("pad_set")
        lists_in = sem("lists_in")
        idx_in = sem("idx_in")
        w_in = sem("w_in")
        consts = sem("consts")
        prep_v = sem("prep_v")
        idx_f = sem("idx_f")
        idx_t = sem("idx_t")
        idx_ready = sem("idx_ready")
        bm_ready = sem("bm_ready")
        w_t = sem("w_t")
        w_tc = sem("w_tc")
        w_c = sem("w_c")
        w_ready = sem("w_ready")

        sp_steps = sem("sp_steps")
        pool_steps = sem("pool_steps")
        staged = sem("staged")
        win_in = sems("win_in", 2)
        same_done = sem("same_done")
        deg_done = sem("deg_done")
        degh_done = sem("degh_done")
        degl_done = sem("degl_done")
        degl_out = sems("degl_out", 2)
        spilled = sems("spilled", RING)
        copied = sems("copied", 2)

        class Round:
            def __init__(self, p):
                self.src_in = sems(f"src_in_{p}_", RING)
                self.dst_in = sems(f"dst_in_{p}_", RING)
                self.turned = sem(f"turned_{p}")
                self.scan_a = sem(f"scan_a_{p}")
                self.scanned = sem(f"scanned_{p}")
                self.hT_ready = sem(f"hT_ready_{p}")
                self.gated = sem(f"gated_{p}")
                self.rz_ready = sem(f"rz_ready_{p}")
                self.rh_done = sem(f"rh_done_{p}")
                self.npre_done = sem(f"npre_done_{p}")
                self.tanh_done = sem(f"tanh_done_{p}")
                self.diff_done = sem(f"diff_done_{p}")
                self.zd_done = sem(f"zd_done_{p}")
                self.updated = sem(f"updated_{p}")

        R1, R2 = Round("1"), Round("2")

        ln_in = sems("ln_in", 4)
        ln_out = sems("ln_out", 4)
        ln_bn = sem("ln_bn")
        ln_sum = sem("ln_sum")
        ln_w = sem("ln_w")
        ln_sd = sem("ln_sd")
        ln_rs = sem("ln_rs")
        ln_coef = sem("ln_coef")
        ln_done = sem("ln_done")

        h1_staged = sem("h1_staged")
        sct_staged = sem("sct_staged")
        scattered = sems("scattered", RING)

        staged2 = sem("staged2")
        rows_in = sems("rows_in", 2)
        xd_in = sems("xd_in", RING)
        y_done = sem("y_done")
        f_bn = sem("f_bn")
        f_sum = sem("f_sum")
        f_w = sem("f_w")
        f_sd = sem("f_sd")
        f_rs = sem("f_rs")
        f_coef = sem("f_coef")
        f_done = sem("f_done")
        out_staged = sem("out_staged")
        final_out = sems("final_out", RING)

        block = ctx.enter_context(nc.Block())

        def known(b):
            return isinstance(b, int)

        def at_least(b, n):
            return not known(b) or b >= n

        def bodies(eng, step, n=BODIES, width=RING):
            for u in range(width):
                step(u, u, 0)
            with eng.Fori(1, n - 1) as i:
                for u in range(width):
                    step(i * width + u, u, i)
            for u in range(width):
                step((n - 1) * width + u, u, n - 1)

        def wait_apart(eng, semaphore, value):
            eng.wait_ge(semaphore, value)
            eng.sem_inc(sp_steps if eng.engine == mybir.EngineType.SP else pool_steps, 1)

        def cols(b):
            return bass.ds(b * SLOTS, SLOTS)

        def ln_rows(ap, s):
            if known(s) and s == LN_FULL:
                return ap[LN_FULL * P * LN_ROWS:N, :].rearrange("(p r) f -> p r f", r=LN_ROWS)
            return ap[bass.ds(s * (P * LN_ROWS), P * LN_ROWS), :].rearrange("(p r) f -> p r f", r=LN_ROWS)

        def ln_p(s):
            return LN_TAIL_P if known(s) and s == LN_FULL else P

        def ln_uses(k, j):
            return (LN_1A // 2 if k < 2 else 0) + j

        @block.sync
        def _(sp):
            sp.dma_start(dst_s[1:1 + E].rearrange("(a n) -> a n", a=8),
                         dst.rearrange("(a n) -> a n", a=8)).then_inc(lists_in, 16)
            sp.dma_start(src_s[0:E].rearrange("(a n) -> a n", a=8),
                         src.rearrange("(a n) -> a n", a=8)).then_inc(lists_in, 16)
            sp.wait_ge(pad_set, 2)
            sp.dma_start(dst_s[0:1].rearrange("(a n) -> a n", a=1), pad_idx[:, 0:1]).then_inc(lists_in, 16)
            sp.dma_start(dst_s[1 + E:EP + 2].rearrange("(a n) -> a n", a=1),
                         pad_idx[:, 0:EP + 1 - E]).then_inc(lists_in, 16)
            sp.dma_start(src_s[E:EP].rearrange("(a n) -> a n", a=1),
                         pad_idx[:, P:P + EP - E]).then_inc(lists_in, 16)
            sp.wait_ge(lists_in, 80)
            for k, (a, o) in enumerate(((dst_s, 1), (dst_s, 2), (src_s, 0))):
                sp.dma_start(raw_idx[k][:, 0:P],
                             a[o:o + P * P].rearrange("(t p) -> t p", p=P)).then_inc(idx_in, 16)
                sp.dma_start(raw_idx[k][0:NT - P, P:2 * P],
                             a[o + P * P:o + NT * P].rearrange("(t p) -> t p", p=P)).then_inc(idx_in, 16)

            def load_window(b, u):
                if at_least(b, 2):
                    sp.wait_ge(same_done, b - 1)
                sp.dma_start(window[u % 2][:, :],
                             dst_s[bass.ds(b * SLOTS, SLOTS + 1)].rearrange("(a n) -> a n", a=1)
                             .broadcast_to([P, SLOTS + 1])).then_inc(win_in[u % 2], 16)

            load_window(0, 0)
            load_window(1, 1)
            for t in range(2):
                sp.dma_start(wmsg_sb[t], W_msg[t].rearrange("(c m) f -> m c f", c=2)).then_inc(w_in, 16)
                sp.dma_start(wih_sb[t], W_ih[t].rearrange("(g m) f -> m g f", g=3)).then_inc(w_in, 16)
                sp.dma_start(whh_sb[t], W_hh[t].rearrange("(g m) f -> m g f", g=3)).then_inc(w_in, 16)
                for c in range(2):
                    sp.dma_start(bm_col[t][:, c:c + 1],
                                 b_msg[t, c * P:(c + 1) * P].rearrange("(p a) -> p a", a=1)).then_inc(w_in, 16)
                sp.dma_start(bih_rep[t][64:96, :],
                             b_ih[t].rearrange("(a n) -> a n", a=1).broadcast_to([32, 3 * P])).then_inc(w_in, 16)
                sp.dma_start(bhh_rep[t][64:96, :],
                             b_hh[t].rearrange("(a n) -> a n", a=1).broadcast_to([32, 3 * P])).then_inc(w_in, 16)

            def copy_chunk(b, u):
                if at_least(b, 2):
                    sp.wait_ge(copied[u % 2], (b - (u % 2)) * 8)
                n = COPY_LAST if known(b) and b == LAST else COPY
                sp.dma_start(h_table[bass.ds(b * COPY, n), :].rearrange("(a r) f -> a (r f)", a=16),
                             x[bass.ds(b * COPY, n), :].rearrange("(a r) f -> a (r f)", a=16))\
                  .then_inc(copied[u % 2], 16)

            def ln_load(s, k, before):
                if not known(before) or before > 0:
                    wait_apart(sp, ln_out[k], before * 16)
                sp.dma_start(lnbuf[k][0:ln_p(s)], ln_rows(x, s)).then_inc(ln_in[k], 16)

            def ln_store(s, k):
                sp.wait_ge(ln_done, s + 1)
                sp.dma_start(ln_rows(out, s), lnbuf[k][0:ln_p(s)]).then_inc(ln_out[k], 16)

            def step(b, u, i):
                if not known(b) or b + 2 <= LAST:
                    load_window(b + 2, u)
                copy_chunk(b, u)
                if u % 2 == 0:
                    if not known(b) or b < LAST:
                        ln_load(2 * i + u // 2, u // 2, i)
                if u == 3:
                    ln_store(2 * i, 0)
                if u == 1 and at_least(i, 1):
                    ln_store(2 * i - 1, 1)
                sp.wait_ge(R1.dst_in[u], (i + 1) * 16 * TILES)
                sp.dma_start(xd_spill[bass.ds(b, 1)].rearrange("a p f -> (a p) f"),
                             dstbuf[u][:, :]).then_inc(spilled[u], 16)
                wait_apart(sp, degl_done, b + 1)
                for r, t in ((0, same[u % 2][0:1, :]), (1, degl[u % 2][0:1, :]), (2, degl[u % 2][32:33, :])):
                    sp.dma_start(rows_spill[r:r + 1, cols(b)], t).then_inc(degl_out[u % 2], 16)
                sp.dma_start(deg_spill[:, cols(b)], degf[u % 2][0:1, :]).then_inc(degl_out[u % 2], 16)

            bodies(sp, step)
            step(LAST, 0, BODIES)
            ln_store(LN_1A - 1, 1)

            def step_b(n, k, j):
                s = n + LN_1A
                ln_load(s, k, ln_uses(k, j))
                if at_least(n, 2):
                    ln_store(s - 2, (k + 2) % 4)

            bodies(sp, step_b, LN_BODIES, 4)
            n = LN_BODIES * 4
            step_b(n, 0, LN_BODIES)
            ln_store(LN_FULL - 1, 3)
            ln_store(LN_FULL, 0)

            sp.wait_ge(degl_out[0], (LAST // 2 + 1) * 64)
            sp.wait_ge(degl_out[1], (LAST // 2) * 64)
            for u in range(RING):
                sp.wait_ge(spilled[u], (BODIES + (u == 0)) * 16)
            for k in range(4):
                sp.wait_ge(ln_out[k], (ln_uses(k, LN_BODIES) + (k == 0)) * 16)
            sp.wait_ge(R1.updated, 2 * NB)

            def rows_load(b, u):
                if at_least(b, 2):
                    sp.wait_ge(R2.gated, 2 * (b - 1))
                sp.dma_start(same[u % 2][:, :], rows_spill[0:1, cols(b)].broadcast_to([P, SLOTS]))\
                  .then_inc(rows_in[u % 2], 16)
                sp.dma_start(deg_rep[u % 2], deg_spill[:, cols(b)].broadcast_to([P, SLOTS]))\
                  .then_inc(rows_in[u % 2], 16)
                for r in (1, 2):
                    sp.dma_start(degl[u % 2][32 * (r - 1):32 * (r - 1) + 3, :],
                                 rows_spill[r:r + 1, cols(b)].broadcast_to([3, SLOTS]))\
                      .then_inc(rows_in[u % 2], 16)

            def xd_load(b, u):
                if at_least(b, RING):
                    sp.wait_ge(y_done, 2 * (b - RING) + 2)
                sp.dma_start(lnbuf[2][:, u * TILES:(u + 1) * TILES, :],
                             xd_spill[bass.ds(b, 1)].rearrange("a p (t f) -> (a p) t f", t=TILES))\
                  .then_inc(xd_in[u], 16)

            def step_2(b, u, i):
                rows_load(b, u)
                xd_load(b, u)

            bodies(sp, step_2)
            step_2(LAST, 0, BODIES)

        @block.gpsimd
        def _(pool):
            nc.gpsimd.memset(pad_idx[:, 0:P], -1).then_inc(pad_set, 1)
            nc.gpsimd.memset(pad_idx[:, P:2 * P], 0).then_inc(pad_set, 1)
            nc.gpsimd.memset(ident[:, :], 0.0).then_inc(consts, 1)
            pool.wait_ge(consts, 1)
            nc.gpsimd.affine_select(out=ident[:, :], in_=ident[:, :], compare_op=ALU.not_equal, fill=1.0,
                                    base=0, pattern=[[-1, P]], channel_multiplier=1).then_inc(consts, 1)
            nc.gpsimd.memset(eps_col[:, :], EPS).then_inc(consts, 1)

            def gather(buf, table, idx, k, done):
                for t in range(TILES):
                    nc.gpsimd.indirect_dma_start(
                        out=buf[:, t * P:(t + 1) * P], out_offset=None, in_=table,
                        in_offset=bass.IndirectOffsetOnAxis(ap=idx[:, k * TILES + t:k * TILES + t + 1], axis=0),
                    ).then_inc(done, 16)

            def scatter(table, buf, idx, t0, done):
                for t in range(TILES):
                    nc.gpsimd.indirect_dma_start(
                        out=table, out_offset=bass.IndirectOffsetOnAxis(ap=idx[:, t:t + 1], axis=0),
                        in_=buf[:, (t0 + t) * P:(t0 + t + 1) * P], in_offset=None,
                        bounds_check=N - 1, oob_is_err=False,
                    ).then_inc(done, 16)

            def step(b, u, i):
                wait_apart(pool, staged, b + 1)
                if at_least(b, RING):
                    wait_apart(pool, R1.turned, b - RING + 1)
                gather(srcbuf[u], x, stage[u], 0, R1.src_in[u])
                if at_least(b, RING):
                    wait_apart(pool, R1.updated, 2 * (b - RING) + 2)
                    wait_apart(pool, spilled[u], i * 16)
                gather(dstbuf[u], x, stage[u], 1, R1.dst_in[u])

            bodies(pool, step)
            step(LAST, 0, BODIES)

            wait_apart(pool, copied[0], (LAST // 2 + 1) * 16)
            wait_apart(pool, copied[1], (LAST // 2) * 16)

            def step_b(b, u, i):
                wait_apart(pool, sct_staged, b + 1)
                wait_apart(pool, h1_staged, b + 1)
                scatter(h_table, srcbuf[u], stage_out[u], 0, scattered[u])

            bodies(pool, step_b)
            step_b(LAST, 0, BODIES)
            for u in range(RING):
                wait_apart(pool, scattered[u], (BODIES + (u == 0)) * 16 * TILES)

            def gather_2(b, u):
                wait_apart(pool, staged2, b + 1)
                if at_least(b, RING):
                    wait_apart(pool, R2.turned, b - RING + 1)
                gather(srcbuf[u], h_table, stage[u], 0, R2.src_in[u])

            def scatter_2(b, u):
                wait_apart(pool, out_staged, b + 1)
                wait_apart(pool, f_done, b + 1)
                scatter(out, lnbuf[0][:, :, :].rearrange("p r f -> p (r f)"), stage_out[u],
                        TILES * u, final_out[u])

            for k in range(4):
                wait_apart(pool, ln_out[k], (ln_uses(k, LN_BODIES) + (k == 0)) * 16)

            def step_2(b, u, i):
                gather_2(b, u)
                if at_least(b, LAG):
                    scatter_2(b - LAG, (u - LAG) % RING)

            bodies(pool, step_2)
            step_2(LAST, 0, BODIES)
            for b in range(LAST - LAG + 1, LAST + 1):
                scatter_2(b, b % RING)
            for u in range(RING):
                wait_apart(pool, final_out[u], (BODIES + (u == 0)) * 16 * TILES)

        @block.tensor
        def _(pe):
            pe.wait_ge(consts, 2)
            pe.wait_ge(idx_f, 1)
            for k, f in enumerate((f_idx[2], f_idx[0], f_out)):
                for c in range(2):
                    last = nc.tensor.transpose(psG[k % 2][:, k // 2, c * P:(c + 1) * P], f[:, c * P:(c + 1) * P],
                                               ident[:, :])
            last.then_inc(idx_t, 1)
            pe.wait_ge(w_in, 2 * 7 * 16)
            pe.wait_ge(idx_ready, 1)
            for t in range(2):
                for c in range(2):
                    for o, g in enumerate((2, 0, 1)):
                        nc.tensor.transpose((psS if c == 0 else psD)[t][:, o * P:(o + 1) * P],
                                            wih_sb[t][:, g, c * P:(c + 1) * P], ident[:, :])
                for g in range(3):
                    last = nc.tensor.transpose(psG[t][:, 0, g * P:(g + 1) * P], whh_sb[t][:, g, :], ident[:, :])
            last.then_inc(w_t, 1)
            pe.wait_ge(w_tc, 1)
            pe.wait_ge(bm_ready, 1)
            for t in range(2):
                for c in range(2):
                    nc.tensor.matmul(psS[t][:, 0:3 * P], wmsg_sb[t][:, c, 0:P], wihT[t][:, c, :],
                                     start=(c == 0), stop=(c == 1))
                for c in range(2):
                    nc.tensor.matmul(psD[t][:, 0:3 * P], wmsg_sb[t][:, c, P:2 * P], wihT[t][:, c, :],
                                     start=(c == 0), stop=(c == 1))
                for c in range(2):
                    last = nc.tensor.matmul(psG[t][0:96, 1, 0:3 * P], bm_rep[t][:, c, :], wihT[t][:, c, :],
                                            start=(c == 0), stop=(c == 1))
            last.then_inc(w_c, 1)
            pe.wait_ge(w_ready, 1)

            def turn(R, b, u, i, src_n, dst_n):
                pe.wait_ge(R.src_in[u], (i + 1) * src_n)
                pe.wait_ge(R.dst_in[u], (i + 1) * dst_n)
                if at_least(b, 2):
                    pe.wait_ge(R.scanned, b - 1)
                    pe.wait_ge(R.hT_ready, b - 1)
                for t in range(TILES):
                    nc.tensor.transpose(psS[u % 2][:, t * P:(t + 1) * P], srcbuf[u][:, t * P:(t + 1) * P], ident[:, :])
                for t in range(TILES):
                    last = nc.tensor.transpose(psD[u % 2][:, t * P:(t + 1) * P], dstbuf[u][:, t * P:(t + 1) * P],
                                               ident[:, :])
                last.then_inc(R.turned, 1)

            def gates(R, w, b, u, rows_ready):
                v = u % 2
                pe.wait_ge(R.scanned, b + 1)
                pe.wait_ge(R.hT_ready, b + 1)
                rows_ready()
                for g in range(2):
                    q = 2 * b + g
                    if at_least(b, 1):
                        pe.wait_ge(R.npre_done, q - 1)
                    for t in range(2):
                        c = slice((2 * g + t) * P, (2 * g + t + 1) * P)
                        G = psG[g][:, t, :]
                        nc.tensor.matmul(G, degl[v][:, c], WB[w][:, :], start=True, stop=False)
                        nc.tensor.matmul(G[:, 0:3 * P], aT[v][:, c], WA[w][:, :], start=False, stop=False)
                        nc.tensor.matmul(G[:, 0:3 * P], dhT[v][:, c], WD[w][:, :], start=False, stop=False)
                        last = nc.tensor.matmul(G[:, P:4 * P], hT[v][:, c], WH[w][:, :], start=False, stop=True)
                    last.then_inc(R.gated, 1)

            def step(b, u, i):
                if not known(b) or b < LAST:
                    turn(R1, b + 1, (u + 1) % RING, i + (u == RING - 1), 16 * TILES, 16 * TILES)
                gates(R1, 0, b, u, lambda: pe.wait_ge(degl_done, b + 1))

            turn(R1, 0, 0, 0, 16 * TILES, 16 * TILES)
            bodies(pe, step)
            step(LAST, 0, BODIES)

            def step_2(b, u, i):
                if not known(b) or b < LAST:
                    turn(R2, b + 1, (u + 1) % RING, i + (u == RING - 1), 16 * TILES, 1)
                gates(R2, 1, b, u, lambda: pe.wait_ge(rows_in[u % 2], (b - u % 2) * 32 + 64))

            turn(R2, 0, 0, 0, 16 * TILES, 1)
            bodies(pe, step_2)
            step_2(LAST, 0, BODIES)

        @block.scalar
        def _(act):
            act.wait_ge(w_t, 1)
            for t in range(2):
                nc.scalar.activation(wihT[t][:, 0, :], psS[t][:, 0:3 * P], ACT.Copy)
                nc.scalar.activation(wihT[t][:, 1, :], psD[t][:, 0:3 * P], ACT.Copy)
                last = nc.scalar.activation(WH[t][:, :], psG[t][:, 0, 0:3 * P], ACT.Copy)
            last.then_inc(w_tc, 1)

            def evac(R, b, u):
                act.wait_ge(R.turned, b + 1)
                if at_least(b, 2):
                    act.wait_ge(R.gated, 2 * (b - 1))
                nc.scalar.activation(hT[u % 2][:, :], psD[u % 2][:, :], ACT.Copy).then_inc(R.hT_ready, 1)

            def nonlinear(R, b):
                for g in range(2):
                    q = 2 * b + g
                    act.wait_ge(R.gated, q + 1)
                    if at_least(b, 1):
                        act.wait_ge(R.updated, q - 1)
                    nc.scalar.activation(rz[g][:, :, :], psG[g][:, :, P:3 * P], ACT.Sigmoid).then_inc(R.rz_ready, 1)
                for g in range(2):
                    act.wait_ge(R.npre_done, 2 * b + g + 1)
                    nc.scalar.activation(nn[g][:, :, :], npre[g][:, :, :], ACT.Tanh).then_inc(R.tanh_done, 1)

            def ln_sqrt(s, v):
                act.wait_ge(ln_w, s + 1)
                nc.scalar.activation(small[v][0:ln_p(s), 4, :], small[v][0:ln_p(s), 3, :], ACT.Sqrt,
                                     bias=eps_col[0:ln_p(s), :]).then_inc(ln_sd, 1)

            def ln_apply(s, k, v):
                act.wait_ge(ln_coef, s + 1)
                n = ln_p(s)
                for r in range(LN_ROWS):
                    last = nc.scalar.activation(lnbuf[k][0:n, r, :], lnbuf[k][0:n, r, :], ACT.Identity,
                                                bias=small[v][0:n, 7, r:r + 1], scale=small[v][0:n, 6, r:r + 1])
                last.then_inc(ln_done, 1)

            def step(b, u, i):
                if not known(b) or b < LAST:
                    evac(R1, b + 1, u + 1)
                nonlinear(R1, b)
                if u % 2 == 1:
                    ln_sqrt(2 * i + u // 2, u // 2)
                elif at_least(b, 2):
                    ln_apply(2 * i + u // 2 - 1, (u // 2 + 1) % 2, (u // 2 + 1) % 2)

            evac(R1, 0, 0)
            bodies(act, step)
            step(LAST, 0, BODIES)

            def stage_h1(b, u, i):
                act.wait_ge(R1.updated, 2 * b + 2)
                if at_least(b, RING):
                    act.wait_ge(scattered[u], i * 16 * TILES)
                else:
                    act.wait_ge(R1.turned, NB)
                nc.scalar.activation(srcbuf[u][:, :], h1[:, cols(b)], ACT.Copy).then_inc(h1_staged, 1)

            def step_b(n, k, j):
                s = n + LN_1A
                if known(n):
                    for b in (2 * n, 2 * n + 1):
                        stage_h1(b, b % RING, b // RING)
                else:
                    for d in range(2):
                        stage_h1(2 * n + d, (2 * k + d) % RING, 2 * j + (2 * k + d) // RING)
                ln_sqrt(s, k % 2)
                if at_least(n, 1):
                    ln_apply(s - 1, (k - 1) % 4, (k - 1) % 2)

            bodies(act, step_b, LN_BODIES, 4)
            stage_h1(LAST, 0, BODIES)
            ln_sqrt(LN_FULL, 0)
            ln_apply(LN_FULL - 1, 3, 1)
            ln_apply(LN_FULL, 0, 0)

            def load_h(b, u):
                if at_least(b, RING):
                    act.wait_ge(R2.updated, 2 * (b - RING) + 2)
                nc.scalar.activation(dstbuf[u][:, :], h1[:, cols(b)], ACT.Copy).then_inc(R2.dst_in[u], 1)

            def f_sqrt(b, v):
                act.wait_ge(f_w, b + 1)
                nc.scalar.activation(small[v][:, 4, 0:TILES], small[v][:, 3, 0:TILES], ACT.Sqrt,
                                     bias=eps_col[:, :], scale=0.25).then_inc(f_sd, 1)

            def f_apply(b, u, v):
                act.wait_ge(f_coef, b + 1)
                y = lnbuf[0]
                for t in range(TILES):
                    r = TILES * u + t
                    last = nc.scalar.activation(y[:, r, :], y[:, r, :], ACT.Identity,
                                                bias=small[v][:, 7, t:t + 1], scale=small[v][:, 5, t:t + 1])
                last.then_inc(f_done, 1)

            for u in range(RING):
                act.wait_ge(spilled[u], (BODIES + (u == 0)) * 16)
            for u in range(RING - 1):
                load_h(u, u)
            evac(R2, 0, 0)

            def step_2(b, u, i):
                if not known(b) or b + RING - 1 <= LAST:
                    load_h(b + RING - 1, (u + RING - 1) % RING)
                if not known(b) or b < LAST:
                    evac(R2, b + 1, u + 1)
                nonlinear(R2, b)
                if at_least(b, 1):
                    f_sqrt(b - 1, (u + 1) % 2)
                    f_apply(b - 1, (u - 1) % RING, (u + 1) % 2)

            bodies(act, step_2)
            step_2(LAST, 0, BODIES)
            f_sqrt(LAST, 0)
            f_apply(LAST, 0, 0)

        @block.vector
        def _(dve):
            links = [0]

            def link(ins):
                links[0] += 1
                ins.then_inc(prep_v, 1)
                dve.wait_ge(prep_v, links[0])

            nc.vector.memset(ones[:, :], 1.0)
            for k in range(2):
                nc.vector.memset(degl[k][0:64, :], 0.0)
                nc.vector.memset(degl[k][64:96, :], 1.0)
                nc.vector.memset(degf[k][:, :], 0.0)
                nc.vector.memset(aT[k][:, :], 0.0)
                nc.vector.memset(dhT[k][:, :], 0.0)
            for k in range(3):
                nc.vector.memset(f_idx[k], 0.0)
            nc.vector.memset(f_same, 0.0)
            link(nc.vector.memset(f_out, 0.0))
            dve.wait_ge(idx_in, 6 * 16)
            for k in range(3):
                nc.vector.tensor_copy(f_idx[k][:, 0:P], raw_idx[k][:, 0:P])
                last = nc.vector.tensor_copy(f_idx[k][0:NT - P, P:2 * P], raw_idx[k][0:NT - P, P:2 * P])
            link(last)
            link(nc.vector.tensor_tensor(f_same, f_idx[0], f_idx[1], ALU.is_equal))
            link(nc.vector.tensor_scalar(f_idx[0], f_idx[0], 0.0, None, ALU.max))
            nc.vector.scalar_tensor_tensor(out=f_out, in0=f_same, scalar=SKIP, in1=f_idx[0],
                                           op0=ALU.mult, op1=ALU.add).then_inc(idx_f, 1)
            dve.wait_ge(idx_t, 1)
            for k in range(3):
                last = nc.vector.tensor_copy(
                    idx_all[:, :, k, :], psG[k % 2][:, k // 2, 0:NT].rearrange("p (b t) -> p b t", t=TILES))
            link(last)

            def stage_idx(b, u, ready, scat=False):
                d, a = (stage_out, slice(2, 3)) if scat else (stage, slice(0, 2))
                nc.vector.tensor_copy(d[u][:, :].rearrange("p (b k t) -> p b k t", b=1, t=TILES),
                                      idx_all[:, bass.ds(b, 1), a, :]).then_inc(ready, 1)

            for u in range(RING):
                stage_idx(u, u, staged)
            dve.wait_ge(consts, 3)
            link(nc.vector.tensor_tensor(sel[:, :], ident[:, 0:3], ident[:, 32:35], ALU.add))
            nc.vector.tensor_tensor(sel[:, :], sel[:, :], ident[:, 64:67], ALU.add).then_inc(idx_ready, 1)

            dve.wait_ge(w_in, 2 * 7 * 16)
            for t in range(2):
                for c in range(2):
                    last = nc.vector.tensor_copy(bm_rep[t][:, c, :], bm_col[t][:, c:c + 1].broadcast_to([P, 96]))
            last.then_inc(bm_ready, 1)
            dve.wait_ge(w_tc, 1)
            dve.wait_ge(idx_ready, 1)
            dve.wait_ge(w_c, 1)
            for t in range(2):
                nc.vector.tensor_copy(WA[t][:, :], psS[t][:, 0:3 * P])
                nc.vector.tensor_copy(WD[t][:, :], psD[t][:, 0:3 * P])
                B, bi, bh = bias_f[t], bih_rep[t], bhh_rep[t]
                nc.vector.tensor_copy(B[0:64, 0:3 * P], psG[t][0:64, 1, 0:3 * P])
                nc.vector.memset(B[0:64, 3 * P:4 * P], 0.0)
                nc.vector.tensor_copy(B[64:96, 0:P], bi[64:96, 2 * P:3 * P])
                nc.vector.tensor_tensor(B[64:96, P:3 * P], bi[64:96, 0:2 * P], bh[64:96, 0:2 * P], ALU.add)
                link(nc.vector.tensor_copy(B[64:96, 3 * P:4 * P], bh[64:96, 2 * P:3 * P]))
                rem = B
                for k in range(3):
                    link(nc.vector.tensor_copy(part[t][k][0:96, :], rem[0:96, :]))
                    if k < 2:
                        link(nc.vector.tensor_tensor(rest[t][k][0:96, :], rem[0:96, :], part[t][k][0:96, :],
                                                     ALU.subtract))
                        rem = rest[t][k]
                link(nc.vector.tensor_scalar(pick[t][0][0:96, :], part[t][0][0:96, :], sel[0:96, 0:1], None, ALU.mult))
                link(nc.vector.scalar_tensor_tensor(out=pick[t][1][0:96, :], in0=part[t][1][0:96, :],
                                                    scalar=sel[0:96, 1:2], in1=pick[t][0][0:96, :],
                                                    op0=ALU.mult, op1=ALU.add))
                last = nc.vector.scalar_tensor_tensor(out=WB[t][:, :], in0=part[t][2][0:96, :],
                                                      scalar=sel[0:96, 2:3], in1=pick[t][1][0:96, :],
                                                      op0=ALU.mult, op1=ALU.add)
            last.then_inc(w_ready, 1)

            def masks(b, u, i):
                v = u % 2
                dve.wait_ge(win_in[v], (b - v) * 8 + 16)
                if at_least(b, 2):
                    dve.wait_ge(degl_out[v], (b - v) * 32)
                    dve.wait_ge(R1.gated, 2 * (b - 1))
                nc.vector.tensor_tensor(same[v][:, :], window[v][:, 1:SLOTS + 1], window[v][:, 0:SLOTS],
                                        ALU.is_equal).then_inc(same_done, 1)
                dve.wait_ge(same_done, b + 1)
                nc.vector.tensor_tensor_scan(degf[v][:, :], same[v][0:64, :], ones[:, :],
                                             degf[1 - v][:, SLOTS - 1:SLOTS], ALU.mult, ALU.add).then_inc(deg_done, 1)
                dve.wait_ge(deg_done, b + 1)
                nc.vector.tensor_copy(degl[v][0:64, :], degf[v][:, :]).then_inc(degh_done, 1)

            def masks_end(b, u):
                v = u % 2
                dve.wait_ge(degh_done, b + 1)
                nc.vector.tensor_tensor(degl[v][32:64, :], degf[v][32:64, :], degl[v][32:64, :],
                                        ALU.subtract).then_inc(degl_done, 1)

            def scans(R, b, u):
                v = u % 2
                dve.wait_ge(R.turned, b + 1)
                if at_least(b, 2):
                    dve.wait_ge(R.gated, 2 * (b - 1))
                if at_least(b, 1):
                    dve.wait_ge(R.scanned, b)
                nc.vector.tensor_tensor_scan(aT[v][:, :], same[v][:, :], psS[v][:, :],
                                             aT[1 - v][:, SLOTS - 1:SLOTS], ALU.mult, ALU.add).then_inc(R.scan_a, 1)
                if at_least(b, 1):
                    dve.wait_ge(R.scan_a, b)
                dve.wait_ge(R.hT_ready, b + 1)
                if R is R1:
                    nc.vector.tensor_tensor_scan(dhT[v][:, :], same[v][:, :], psD[v][:, :],
                                                 dhT[1 - v][:, SLOTS - 1:SLOTS], ALU.mult, ALU.add)\
                      .then_inc(R.scanned, 1)
                else:
                    nc.vector.tensor_tensor(dhT[v][:, :], deg_rep[v], psD[v][:, :], ALU.mult)\
                      .then_inc(R.scanned, 1)

            def candidate(R, b):
                for g in range(2):
                    dve.wait_ge(R.rz_ready, 2 * b + g + 1)
                    nc.vector.tensor_tensor(npre[g][:, :, :], rz[g][:, :, 0:P], psG[g][:, :, 3 * P:4 * P],
                                            ALU.mult).then_inc(R.rh_done, 1)
                for g in range(2):
                    dve.wait_ge(R.rh_done, 2 * b + g + 1)
                    nc.vector.tensor_tensor(npre[g][:, :, :], npre[g][:, :, :], psG[g][:, :, 0:P],
                                            ALU.add).then_inc(R.npre_done, 1)

            def update(R, b, u, to):
                h = dstbuf[u][:, :].rearrange("p (g t f) -> p g t f", g=2, t=2)
                for g in range(2):
                    dve.wait_ge(R.tanh_done, 2 * b + g + 1)
                    nc.vector.tensor_tensor(dd[g][:, :, :], h[:, g], nn[g][:, :, :], ALU.subtract)\
                      .then_inc(R.diff_done, 1)
                for g in range(2):
                    dve.wait_ge(R.diff_done, 2 * b + g + 1)
                    nc.vector.tensor_tensor(dd[g][:, :, :], rz[g][:, :, P:2 * P], dd[g][:, :, :], ALU.mult)\
                      .then_inc(R.zd_done, 1)
                for g in range(2):
                    dve.wait_ge(R.zd_done, 2 * b + g + 1)
                    nc.vector.tensor_tensor(to(g), nn[g][:, :, :], dd[g][:, :, :], ALU.add).then_inc(R.updated, 1)

            def h1_group(b):
                return lambda g: h1[:, bass.ds(b * SLOTS + g * 2 * P, 2 * P)].rearrange("p (t f) -> p t f", t=2)

            def moments(v, n, rows, bn, total, w):
                S, T = small[v], st[v]
                dve.wait_ge(bn[0], bn[1])
                nc.vector.tensor_tensor(S[0:n, 0, 0:rows], T[0:n, 0:rows, 1], T[0:n, 0:rows, 4], ALU.add)
                nc.vector.tensor_tensor(S[0:n, 1, 0:rows], T[0:n, 0:rows, 1], T[0:n, 0:rows, 4], ALU.subtract)
                nc.vector.tensor_tensor(S[0:n, 2, 0:rows], T[0:n, 0:rows, 2], T[0:n, 0:rows, 5], ALU.add)\
                  .then_inc(total[0], 1)
                dve.wait_ge(total[0], 2 * total[1] - 1)
                nc.vector.tensor_tensor(S[0:n, 1, 0:rows], S[0:n, 1, 0:rows], S[0:n, 1, 0:rows], ALU.mult)\
                  .then_inc(total[0], 1)
                dve.wait_ge(total[0], 2 * total[1])
                nc.vector.scalar_tensor_tensor(out=S[0:n, 3, 0:rows], in0=S[0:n, 2, 0:rows], scalar=4.0 / P,
                                               in1=S[0:n, 1, 0:rows], op0=ALU.mult, op1=ALU.add).then_inc(w, 1)

            def ln_stats(s, k, v, use):
                n = ln_p(s)
                dve.wait_ge(ln_in[k], (use + 1) * 16)
                if at_least(s, 2):
                    dve.wait_ge(ln_done, s - 1)
                for r in range(LN_ROWS):
                    last = nc.vector.bn_stats(st[v][0:n, r, :], lnbuf[k][0:n, r, :])
                last.then_inc(ln_bn, 1)
                moments(v, n, LN_ROWS, (ln_bn, s + 1), (ln_sum, s + 1), ln_w)

            def ln_finish(s, v):
                n, S = ln_p(s), small[v]
                dve.wait_ge(ln_sd, s + 1)
                nc.vector.reciprocal(S[0:n, 5, :], S[0:n, 4, :]).then_inc(ln_rs, 1)
                dve.wait_ge(ln_rs, s + 1)
                nc.vector.tensor_scalar(S[0:n, 6, :], S[0:n, 5, :], 2.0, None, ALU.mult)
                nc.vector.scalar_tensor_tensor(out=S[0:n, 7, :], in0=S[0:n, 0, :], scalar=-1.0, in1=S[0:n, 5, :],
                                               op0=ALU.mult, op1=ALU.mult).then_inc(ln_coef, 1)

            def step(b, u, i):
                if not known(b) or b + RING <= LAST:
                    dve.wait_ge(R1.src_in[u], (i + 1) * 16 * TILES)
                    dve.wait_ge(R1.dst_in[u], (i + 1) * 16 * TILES)
                    stage_idx(b + RING, u, staged)
                if not known(b) or b < LAST:
                    masks(b + 1, u + 1, i)
                candidate(R1, b)
                if not known(b) or b < LAST:
                    masks_end(b + 1, u + 1)
                    scans(R1, b + 1, u + 1)
                update(R1, b, u, h1_group(b))
                if u % 2 == 1:
                    ln_stats(2 * i + u // 2, u // 2, u // 2, i)
                elif at_least(b, 2):
                    ln_finish(2 * i + u // 2 - 1, (u // 2 + 1) % 2)

            dve.wait_ge(w_ready, 1)
            masks(0, 0, 0)
            masks_end(0, 0)
            scans(R1, 0, 0)
            bodies(dve, step)
            step(LAST, 0, BODIES)

            def stage_sct(b, u, i):
                if at_least(b, RING):
                    dve.wait_ge(scattered[u], i * 16 * TILES)
                stage_idx(b, u, sct_staged, scat=True)

            def step_b(n, k, j):
                s = n + LN_1A
                if known(n):
                    for b in (2 * n, 2 * n + 1):
                        stage_sct(b, b % RING, b // RING)
                else:
                    for d in range(2):
                        stage_sct(2 * n + d, (2 * k + d) % RING, 2 * j + (2 * k + d) // RING)
                ln_stats(s, k, k % 2, ln_uses(k, j))
                if at_least(n, 1):
                    ln_finish(s - 1, (k - 1) % 2)

            bodies(dve, step_b, LN_BODIES, 4)
            stage_sct(LAST, 0, BODIES)
            ln_stats(LN_FULL, 0, 0, ln_uses(0, LN_BODIES))
            ln_finish(LN_FULL - 1, 1)
            ln_finish(LN_FULL, 0)

            for u in range(RING):
                stage_idx(u, u, staged2)
            dve.wait_ge(R1.scanned, NB)
            for k in range(2):
                last = nc.vector.memset(aT[k][:, SLOTS - 1:SLOTS], 0.0)
            link(last)
            for u in range(RING):
                dve.wait_ge(scattered[u], (BODIES + (u == 0)) * 16 * TILES)
            dve.wait_ge(ln_done, LN_FULL + 1)

            def rows(b, u):
                dve.wait_ge(rows_in[u % 2], (b - u % 2) * 32 + 64)

            def residual(b, u):
                y = lnbuf[0]
                dve.wait_ge(xd_in[u], ((b - u) // RING + 1) * 16 if known(b) else (b - u) * (16 // RING) + 16)
                for g in range(2):
                    dve.wait_ge(R2.updated, 2 * b + g + 1)
                    last = nc.vector.tensor_tensor(
                        y[:, TILES * u + 2 * g:TILES * u + 2 * g + 2, :], hout[g][:, :, :],
                        lnbuf[2][:, TILES * u + 2 * g:TILES * u + 2 * g + 2, :], ALU.add)
                    last.then_inc(y_done, 1)
                dve.wait_ge(y_done, 2 * b + 2)
                if at_least(b, 2):
                    dve.wait_ge(f_done, b - 1)
                for t in range(TILES):
                    last = nc.vector.bn_stats(st[u % 2][:, t, :], y[:, TILES * u + t, :])
                last.then_inc(f_bn, 1)
                moments(u % 2, P, TILES, (f_bn, b + 1), (f_sum, b + 1), f_w)

            def finish(b, v):
                S = small[v]
                dve.wait_ge(f_sd, b + 1)
                nc.vector.reciprocal(S[:, 5, 0:TILES], S[:, 4, 0:TILES]).then_inc(f_rs, 1)
                dve.wait_ge(f_rs, b + 1)
                nc.vector.scalar_tensor_tensor(out=S[:, 7, 0:TILES], in0=S[:, 0, 0:TILES], scalar=-0.5,
                                               in1=S[:, 5, 0:TILES], op0=ALU.mult, op1=ALU.mult).then_inc(f_coef, 1)

            def step_2(b, u, i):
                if not known(b) or b + RING <= LAST:
                    dve.wait_ge(R2.src_in[u], (i + 1) * 16 * TILES)
                    stage_idx(b + RING, u, staged2)
                if at_least(b, RING):
                    dve.wait_ge(final_out[u], i * 16 * TILES)
                stage_idx(b, u, out_staged, scat=True)
                candidate(R2, b)
                if not known(b) or b < LAST:
                    rows(b + 1, u + 1)
                    scans(R2, b + 1, u + 1)
                update(R2, b, u, lambda g: hout[g][:, :, :])
                if at_least(b, 1):
                    finish(b - 1, (u + 1) % 2)
                residual(b, u)

            rows(0, 0)
            scans(R2, 0, 0)
            bodies(dve, step_2)
            step_2(LAST, 0, BODIES)
            finish(LAST, 0)


_INS = ["x", "src", "dst", "L0_gnn_W_msg", "L0_gnn_b_msg", "L0_gnn_W_ih", "L0_gnn_W_hh", "L0_gnn_b_ih", "L0_gnn_b_hh"]


def kernel(**inputs):
    import numpy as np
    import concourse.bacc as bacc
    from concourse import mybir as mb
    from concourse.bass_utils import run_bass_kernel_spmd as run

    nc = bacc.Bacc("TRN2", target_bir_lowering=False, num_devices=1)
    arrays, args = {}, []
    for name in _INS:
        a = np.ascontiguousarray(inputs[name])
        arrays[f"in_{name}"] = a
        args.append(nc.dram_tensor(f"in_{name}", a.shape, mb.dt.from_np(a.dtype), kind="ExternalInput").ap())
    out = nc.dram_tensor("out_rows", arrays["in_x"].shape, mb.dt.float32, kind="ExternalOutput").ap()
    build(nc, *args, out)
    r = run(nc, [arrays], core_ids=[0])
    return r.results[0]["out_rows"]
```

```python
from contextlib import ExitStack

import concourse.bass as bass
from concourse import mybir

P = 128
TILES = 4
SLOTS = P * TILES
RING = 4
WIDE = 8
LAG = 4
APPLY_LAG = 7
LN_ROWS = 16
SKIP = float(1 << 20)
EPS = 1e-5

F32 = mybir.dt.float32
BF16 = mybir.dt.bfloat16
I32 = mybir.dt.int32
ALU = mybir.AluOpType
ACT = mybir.ActivationFunctionType


def build(nc, x, src, dst, W_msg, b_msg, W_ih, W_hh, b_ih, b_hh, out):
    N, H = x.shape
    E = src.shape[0]
    assert H == P and W_msg.shape[0] == 2
    NB = -(-E // SLOTS)
    NT = NB * TILES
    EP = NB * SLOTS
    BODIES = (NB - 1) // WIDE
    assert NB == BODIES * WIDE + 1 and BODIES >= 4
    LAST = NB - 1
    LN_FULL = N // (P * LN_ROWS)
    LN_TAIL_P = (N - LN_FULL * P * LN_ROWS) // LN_ROWS
    assert LN_TAIL_P * LN_ROWS + LN_FULL * P * LN_ROWS == N and 0 < LN_TAIL_P < P
    LN_1A = 4 * BODIES
    LN_BODIES = (LN_FULL - LN_1A) // 4
    assert LN_1A + 4 * LN_BODIES == LN_FULL and LN_BODIES == BODIES
    COPY = -(-N // (NB * 16)) * 16
    COPY_LAST = N - COPY * LAST
    assert 0 < COPY_LAST <= COPY
    GATES = 4 * P

    ctx = ExitStack()
    with ctx:
        def sb(name, shape, dt=F32):
            return ctx.enter_context(nc.sbuf_tensor(name, shape, dt))

        def sem(name):
            return ctx.enter_context(nc.semaphore(name))

        def sems(name, n):
            return [sem(f"{name}{k}") for k in range(n)]

        dst_s = nc.dram_tensor("dst_s", [EP + 2], I32, kind="Internal").ap()
        src_s = nc.dram_tensor("src_s", [EP], I32, kind="Internal").ap()
        h_table = nc.dram_tensor("h_table", [N, P], F32, kind="Internal").ap()
        xd_spill = nc.dram_tensor("xd_spill", [NB, P, SLOTS], F32, kind="Internal").ap()
        rows_d = nc.dram_tensor("rows_d", [3, EP], BF16, kind="Internal").ap()

        deg_d = nc.dram_tensor("deg_d", [1, EP], F32, kind="Internal").ap()

        h1 = sb("h1", [P, EP])
        srcbuf = [sb(f"srcbuf{k}", [P, SLOTS]) for k in range(RING)]
        dstbuf = [sb(f"dstbuf{k}", [P, SLOTS]) for k in range(RING)]
        lnbuf = [sb(f"lnbuf{k}", [P, LN_ROWS, P]) for k in range(4)]
        aT = [sb(f"aT{k}", [P, SLOTS]) for k in range(2)]
        dhT = [sb(f"dhT{k}", [P, SLOTS]) for k in range(2)]
        hT = [sb(f"hT{k}", [P, SLOTS]) for k in range(2)]
        rz = [sb(f"rz{k}", [P, 2, 2 * P]) for k in range(2)]
        npre = [sb(f"npre{k}", [P, 2, P]) for k in range(2)]
        nn = [sb(f"nn{k}", [P, 2, P]) for k in range(2)]
        dd = [sb(f"dd{k}", [P, 2, P]) for k in range(2)]
        hout = [sb(f"hout{k}", [P, 2, P]) for k in range(2)]
        same = [sb(f"same{k}", [P, SLOTS], BF16) for k in range(RING)]
        degl = [sb(f"degl{k}", [96, SLOTS], BF16) for k in range(RING)]
        idx_all = sb("idx_all", [P, NB, 3, TILES], I32)
        stage = [sb(f"stage{k}", [P, 2 * TILES], I32) for k in range(RING)]
        stage_out = [sb(f"stage_out{k}", [P, TILES], I32) for k in range(WIDE)]
        WA = [sb(f"WA{t}", [P, 3 * P]) for t in range(2)]
        WD = [sb(f"WD{t}", [P, 3 * P]) for t in range(2)]
        WH = [sb(f"WH{t}", [P, 3 * P]) for t in range(2)]
        WB = [sb(f"WB{t}", [96, GATES], BF16) for t in range(2)]
        ident = sb("ident", [P, P])
        sel = sb("sel", [P, 3])
        eps_col = sb("eps_col", [P, 1])
        st = [sb(f"st{k}", [P, LN_ROWS, 6]) for k in range(2)]
        small = [sb(f"small{k}", [P, 8, LN_ROWS]) for k in range(2)]
        pad_idx = sb("pad_idx", [1, 2 * P], I32)

        psS = [ctx.enter_context(nc.psum_tensor(f"psS{k}", [P, SLOTS], F32)) for k in range(2)]
        psD = [ctx.enter_context(nc.psum_tensor(f"psD{k}", [P, SLOTS], F32)) for k in range(2)]
        psG = [ctx.enter_context(nc.psum_tensor(f"psG{k}", [P, 2, GATES], F32)) for k in range(2)]

        def y_rows(u):
            return lnbuf[u // 4][:, TILES * (u % 4):TILES * (u % 4) + TILES, :]

        deg_rep = [lnbuf[3][:, TILES * k:TILES * (k + 1), :].rearrange("p t f -> p (t f)") for k in range(RING)]

        off = [0]

        def over_h1(cols, dt=F32):
            a = h1[:, off[0]:off[0] + cols]
            off[0] += cols
            return a if dt is F32 else a.bitcast(dt)

        raw_idx = [over_h1(2 * P, I32) for _ in range(4)]
        f_idx = [over_h1(2 * P) for _ in range(4)]
        f_same = over_h1(2 * P)
        f_out = over_h1(2 * P)
        f_node, f_prev, f_head, f_local, f_deg = (over_h1(2 * P) for _ in range(5))
        ones_f = over_h1(2 * P)
        ends = over_h1(4 * P)
        carry = over_h1(2 * P + 2)
        carry_col = over_h1(2)
        b_same, b_hi, b_lo = (over_h1(P, BF16) for _ in range(3))
        wmsg_sb = [over_h1(2 * 2 * P).rearrange("p (c f) -> p c f", c=2) for _ in range(2)]
        wih_sb = [over_h1(3 * 2 * P).rearrange("p (g f) -> p g f", g=3) for _ in range(2)]
        whh_sb = [over_h1(3 * P).rearrange("p (g f) -> p g f", g=3) for _ in range(2)]
        wihT = [over_h1(2 * 3 * P).rearrange("p (c g) -> p c g", c=2) for _ in range(2)]
        bm_col = [over_h1(2) for _ in range(2)]
        bm_rep = [over_h1(2 * 96).rearrange("p (c r) -> p c r", c=2) for _ in range(2)]
        bih_rep = [over_h1(3 * P) for _ in range(2)]
        bhh_rep = [over_h1(3 * P) for _ in range(2)]
        bias_f = [over_h1(GATES) for _ in range(2)]
        part = [[over_h1(GATES // 2, BF16) for _ in range(3)] for _ in range(2)]
        rest = [[over_h1(GATES) for _ in range(2)] for _ in range(2)]
        pick = [[over_h1(GATES) for _ in range(3)] for _ in range(2)]
        assert off[0] <= EP

        pad_set = sem("pad_set")
        lists_in = sem("lists_in")
        idx_in = sem("idx_in")
        w_in = sem("w_in")
        consts = sem("consts")
        prep_v = sem("prep_v")
        idx_f = sem("idx_f")
        idx_t = sem("idx_t")
        idx_ready = sem("idx_ready")
        bm_ready = sem("bm_ready")
        w_t = sem("w_t")
        w_tc = sem("w_tc")
        w_c = sem("w_c")
        w_ready = sem("w_ready")

        sp_steps = sem("sp_steps")
        pool_steps = sem("pool_steps")
        staged = sem("staged")
        ends_ready = sem("ends_ready")
        ends_row = sem("ends_row")
        carry_row = sem("carry_row")
        carry_in = sem("carry_in")
        deg_ready = sem("deg_ready")
        deg_out = sem("deg_out")
        spilled = sems("spilled", RING)
        copied = sems("copied", 2)

        class Round:
            def __init__(self, p):
                self.src_in = sems(f"src_in_{p}_", RING)
                self.dst_in = sems(f"dst_in_{p}_", RING)
                self.rows_in = sems(f"rows_in_{p}_", RING)
                self.turned = sem(f"turned_{p}")
                self.scan_a = sem(f"scan_a_{p}")
                self.scanned = sem(f"scanned_{p}")
                self.hT_ready = sem(f"hT_ready_{p}")
                self.gated = sem(f"gated_{p}")
                self.rz_ready = sem(f"rz_ready_{p}")
                self.rh_done = sem(f"rh_done_{p}")
                self.npre_done = sem(f"npre_done_{p}")
                self.tanh_done = sem(f"tanh_done_{p}")
                self.diff_done = sem(f"diff_done_{p}")
                self.zd_done = sem(f"zd_done_{p}")
                self.updated = sem(f"updated_{p}")

        R1, R2 = Round("1"), Round("2")

        ln_in = sems("ln_in", 4)
        ln_out = sems("ln_out", 4)
        ln_bn = sem("ln_bn")
        ln_sum = sem("ln_sum")
        ln_w = sem("ln_w")
        ln_sd = sem("ln_sd")
        ln_rs = sem("ln_rs")
        ln_coef = sem("ln_coef")
        ln_done = sem("ln_done")

        h1_staged = sem("h1_staged")
        sct_staged = sem("sct_staged")
        scattered = sems("scattered", RING)

        staged2 = sem("staged2")
        
        xd_in = sems("xd_in", RING)
        y_done = sem("y_done")
        f_bn = sem("f_bn")
        f_sum = sem("f_sum")
        f_w = sem("f_w")
        f_sd = sem("f_sd")
        f_rs = sem("f_rs")
        f_coef = sem("f_coef")
        f_done = sem("f_done")
        out_staged = sem("out_staged")
        final_out = sems("final_out", WIDE)

        block = ctx.enter_context(nc.Block())

        def known(b):
            return isinstance(b, int)

        def at_least(b, n):
            return not known(b) or b >= n

        def bodies(eng, step):
            for u in range(WIDE):
                step(u, u, 0)
            with eng.Fori(1, BODIES - 1) as i:
                for u in range(WIDE):
                    step(i * WIDE + u, u, i)
            for u in range(WIDE):
                step((BODIES - 1) * WIDE + u, u, BODIES - 1)

        def ln_bodies(eng, step):
            for k in range(4):
                step(LN_1A + k, k, BODIES)
            with eng.Fori(1, LN_BODIES) as j:
                for k in range(4):
                    step(j * 4 + LN_1A + k, k, j + BODIES)

        def uses(u, i):
            return i * (WIDE // RING) + u // RING

        def wait_apart(eng, semaphore, value):
            eng.wait_ge(semaphore, value)
            eng.sem_inc(sp_steps if eng.engine == mybir.EngineType.SP else pool_steps, 1)

        def cols(b):
            return bass.ds(b * SLOTS, SLOTS)

        def ln_rows(ap, s):
            if known(s) and s == LN_FULL:
                return ap[LN_FULL * P * LN_ROWS:N, :].rearrange("(p r) f -> p r f", r=LN_ROWS)
            return ap[bass.ds(s * (P * LN_ROWS), P * LN_ROWS), :].rearrange("(p r) f -> p r f", r=LN_ROWS)

        def ln_p(s):
            return LN_TAIL_P if known(s) and s == LN_FULL else P

        @block.sync
        def _(sp):
            sp.dma_start(dst_s[1:1 + E].rearrange("(a n) -> a n", a=8),
                         dst.rearrange("(a n) -> a n", a=8)).then_inc(lists_in, 16)
            sp.dma_start(src_s[0:E].rearrange("(a n) -> a n", a=8),
                         src.rearrange("(a n) -> a n", a=8)).then_inc(lists_in, 16)
            sp.wait_ge(pad_set, 2)
            sp.dma_start(dst_s[0:1].rearrange("(a n) -> a n", a=1), pad_idx[:, 0:1]).then_inc(lists_in, 16)
            sp.dma_start(dst_s[1 + E:EP + 2].rearrange("(a n) -> a n", a=1),
                         pad_idx[:, 0:EP + 1 - E]).then_inc(lists_in, 16)
            sp.dma_start(src_s[E:EP].rearrange("(a n) -> a n", a=1),
                         pad_idx[:, P:P + EP - E]).then_inc(lists_in, 16)
            sp.wait_ge(lists_in, 80)
            for k, (a, o) in enumerate(((dst_s, 1), (dst_s, 2), (src_s, 0), (dst_s, 0))):
                sp.dma_start(raw_idx[k][:, 0:P],
                             a[o:o + P * P].rearrange("(t p) -> t p", p=P)).then_inc(idx_in, 16)
                sp.dma_start(raw_idx[k][0:NT - P, P:2 * P],
                             a[o + P * P:o + NT * P].rearrange("(t p) -> t p", p=P)).then_inc(idx_in, 16)
            for t in range(2):
                sp.dma_start(wmsg_sb[t], W_msg[t].rearrange("(c m) f -> m c f", c=2)).then_inc(w_in, 16)
                sp.dma_start(wih_sb[t], W_ih[t].rearrange("(g m) f -> m g f", g=3)).then_inc(w_in, 16)
                sp.dma_start(whh_sb[t], W_hh[t].rearrange("(g m) f -> m g f", g=3)).then_inc(w_in, 16)
                for c in range(2):
                    sp.dma_start(bm_col[t][:, c:c + 1],
                                 b_msg[t, c * P:(c + 1) * P].rearrange("(p a) -> p a", a=1)).then_inc(w_in, 16)
                sp.dma_start(bih_rep[t][64:96, :],
                             b_ih[t].rearrange("(a n) -> a n", a=1).broadcast_to([32, 3 * P])).then_inc(w_in, 16)
                sp.dma_start(bhh_rep[t][64:96, :],
                             b_hh[t].rearrange("(a n) -> a n", a=1).broadcast_to([32, 3 * P])).then_inc(w_in, 16)

            sp.wait_ge(deg_ready, 1)
            for k, t in enumerate((b_same, b_hi, b_lo)):
                sp.dma_start(rows_d[k, 0:P * P].rearrange("(t p) -> t p", p=P), t[:, 0:P]).then_inc(deg_out, 16)
                sp.dma_start(rows_d[k, P * P:EP].rearrange("(t p) -> t p", p=P),
                             t[0:NT - P, P:2 * P]).then_inc(deg_out, 16)
            sp.dma_start(deg_d[0, 0:P * P].rearrange("(t p) -> t p", p=P), f_deg[:, 0:P]).then_inc(deg_out, 16)
            sp.dma_start(deg_d[0, P * P:EP].rearrange("(t p) -> t p", p=P),
                         f_deg[0:NT - P, P:2 * P]).then_inc(deg_out, 16)
            sp.wait_ge(deg_out, 8 * 16)

            def rows_load(R, b, u):
                k = u % RING
                if at_least(b, RING):
                    sp.wait_ge(R.gated, 2 * (b - RING) + 2)
                sp.dma_start(same[k][:, :], rows_d[0:1, cols(b)].broadcast_to([P, SLOTS]))\
                  .then_inc(R.rows_in[k], 16)
                for r in (1, 2):
                    sp.dma_start(degl[k][32 * (r - 1):32 * (r - 1) + 3, :],
                                 rows_d[r:r + 1, cols(b)].broadcast_to([3, SLOTS])).then_inc(R.rows_in[k], 16)
                if R is R2:
                    sp.dma_start(deg_rep[k], deg_d[:, cols(b)].broadcast_to([P, SLOTS])).then_inc(R.rows_in[k], 16)

            def copy_chunk(b, u):
                if at_least(b, 2):
                    wait_apart(sp, copied[u % 2], (b - (u % 2)) * 8)
                n = COPY_LAST if known(b) and b == LAST else COPY
                sp.dma_start(h_table[bass.ds(b * COPY, n), :].rearrange("(a r) f -> a (r f)", a=16),
                             x[bass.ds(b * COPY, n), :].rearrange("(a r) f -> a (r f)", a=16))\
                  .then_inc(copied[u % 2], 16)

            def ln_load(s, k, before):
                if not known(before) or before > 0:
                    wait_apart(sp, ln_out[k], before * 16)
                sp.dma_start(lnbuf[k][0:ln_p(s)], ln_rows(x, s)).then_inc(ln_in[k], 16)

            def ln_store(s, k):
                sp.wait_ge(ln_done, s + 1)
                sp.dma_start(ln_rows(out, s), lnbuf[k][0:ln_p(s)]).then_inc(ln_out[k], 16)

            def step(b, u, i):
                if not known(b) or b + 2 <= LAST:
                    rows_load(R1, b + 2, u + 2)
                copy_chunk(b, u)
                if u % 2 == 1 and (not known(b) or b // 2 + 1 < LN_1A):
                    ln_load(4 * i + u // 2 + 1, (u // 2 + 1) % 4, i + (u == WIDE - 1))
                if u % 2 == 0 and at_least(b, 6):
                    ln_store(4 * i + u // 2 - 3, (u // 2 + 1) % 4)
                sp.wait_ge(R1.dst_in[u % RING], (uses(u, i) + 1) * 16 * TILES)
                sp.dma_start(xd_spill[bass.ds(b, 1)].rearrange("a p f -> (a p) f"),
                             dstbuf[u % RING][:, :]).then_inc(spilled[u % RING], 16)

            rows_load(R1, 0, 0)
            rows_load(R1, 1, 1)
            ln_load(0, 0, 0)
            bodies(sp, step)
            step(LAST, 0, BODIES)
            for g in range(LN_1A - 2, LN_1A):
                ln_store(g, g % 4)

            def step_b(s, k, before):
                ln_load(s, k, before)
                if at_least(s, LN_1A + 2):
                    ln_store(s - 2, (k + 2) % 4)

            ln_bodies(sp, step_b)
            step_b(LN_FULL, 0, BODIES + LN_BODIES)
            ln_store(LN_FULL - 1, 3)
            ln_store(LN_FULL, 0)

            for u in range(RING):
                sp.wait_ge(spilled[u], (uses(0, BODIES) + (u == 0)) * 16)
            for k in range(4):
                sp.wait_ge(ln_out[k], (BODIES + LN_BODIES + (k == 0)) * 16)
            sp.wait_ge(R1.updated, 2 * NB)

            def xd_load(b, u):
                k = u % RING
                if at_least(b, RING):
                    sp.wait_ge(y_done, 2 * (b - RING) + 2)
                sp.dma_start(lnbuf[2][:, k * TILES:(k + 1) * TILES, :],
                             xd_spill[bass.ds(b, 1)].rearrange("a p (t f) -> (a p) t f", t=TILES))\
                  .then_inc(xd_in[k], 16)

            def step_2(b, u, i):
                rows_load(R2, b, u)
                xd_load(b, u)

            bodies(sp, step_2)
            step_2(LAST, 0, BODIES)

        @block.gpsimd
        def _(pool):
            nc.gpsimd.memset(pad_idx[:, 0:P], -1).then_inc(pad_set, 1)
            nc.gpsimd.memset(pad_idx[:, P:2 * P], 0).then_inc(pad_set, 1)
            nc.gpsimd.memset(ident[:, :], 0.0).then_inc(consts, 1)
            pool.wait_ge(consts, 1)
            nc.gpsimd.affine_select(out=ident[:, :], in_=ident[:, :], compare_op=ALU.not_equal, fill=1.0,
                                    base=0, pattern=[[-1, P]], channel_multiplier=1).then_inc(consts, 1)
            nc.gpsimd.memset(eps_col[:, :], EPS).then_inc(consts, 1)

            def gather(buf, table, idx, k, done):
                for t in range(TILES):
                    nc.gpsimd.indirect_dma_start(
                        out=buf[:, t * P:(t + 1) * P], out_offset=None, in_=table,
                        in_offset=bass.IndirectOffsetOnAxis(ap=idx[:, k * TILES + t:k * TILES + t + 1], axis=0),
                    ).then_inc(done, 16)

            def scatter(table, buf, idx, t0, done):
                for t in range(TILES):
                    nc.gpsimd.indirect_dma_start(
                        out=table, out_offset=bass.IndirectOffsetOnAxis(ap=idx[:, t:t + 1], axis=0),
                        in_=buf[:, (t0 + t) * P:(t0 + t + 1) * P], in_offset=None,
                        bounds_check=N - 1, oob_is_err=False,
                    ).then_inc(done, 16)

            def step(b, u, i):
                k = u % RING
                wait_apart(pool, staged, b + 1)
                if at_least(b, RING):
                    wait_apart(pool, R1.turned, b - RING + 1)
                gather(srcbuf[k], x, stage[k], 0, R1.src_in[k])
                if at_least(b, RING):
                    wait_apart(pool, R1.updated, 2 * (b - RING) + 2)
                    wait_apart(pool, spilled[k], uses(u, i) * 16)
                gather(dstbuf[k], x, stage[k], 1, R1.dst_in[k])

            bodies(pool, step)
            step(LAST, 0, BODIES)

            pool.wait_ge(copied[0], (LAST // 2 + 1) * 16)
            pool.wait_ge(copied[1], (LAST // 2) * 16)

            def step_b(b, u, i):
                wait_apart(pool, sct_staged, b + 1)
                wait_apart(pool, h1_staged, b + 1)
                scatter(h_table, srcbuf[u % RING], stage_out[u % RING], 0, scattered[u % RING])

            bodies(pool, step_b)
            step_b(LAST, 0, BODIES)
            for u in range(RING):
                pool.wait_ge(scattered[u], (uses(0, BODIES) + (u == 0)) * 16 * TILES)

            def gather_2(b, u):
                wait_apart(pool, staged2, b + 1)
                if at_least(b, RING):
                    wait_apart(pool, R2.turned, b - RING + 1)
                gather(srcbuf[u % RING], h_table, stage[u % RING], 0, R2.src_in[u % RING])

            def scatter_2(b, u):
                wait_apart(pool, out_staged, b + 1)
                wait_apart(pool, f_done, b + 1)
                scatter(out, y_rows(u).rearrange("p r f -> p (r f)"), stage_out[u], 0, final_out[u])

            for k in range(4):
                pool.wait_ge(ln_out[k], (BODIES + LN_BODIES + (k == 0)) * 16)

            def step_2(b, u, i):
                gather_2(b, u)
                if at_least(b, LAG):
                    scatter_2(b - LAG, (u - LAG) % WIDE)

            bodies(pool, step_2)
            step_2(LAST, 0, BODIES)
            for b in range(LAST - LAG + 1, LAST + 1):
                scatter_2(b, b % WIDE)
            for u in range(WIDE):
                pool.wait_ge(final_out[u], (BODIES + (u == 0)) * 16 * TILES)

        @block.tensor
        def _(pe):
            pe.wait_ge(consts, 2)
            pe.wait_ge(idx_f, 1)
            for k, f in enumerate((f_idx[2], f_node, f_out)):
                for c in range(2):
                    last = nc.tensor.transpose(psG[k % 2][:, k // 2, c * P:(c + 1) * P], f[:, c * P:(c + 1) * P],
                                               ident[:, :])
            last.then_inc(idx_t, 1)
            pe.wait_ge(ends_ready, 1)
            pe.wait_ge(idx_ready, 1)
            for k, f in enumerate((f_local, f_head)):
                for c in range(2):
                    last = nc.tensor.matmul(psS[0][0:1, (2 * k + c) * P:(2 * k + c + 1) * P],
                                            f[:, c * P + P - 1:c * P + P], ident[:, :], start=True, stop=True)
            last.then_inc(ends_row, 1)
            pe.wait_ge(carry_row, 1)
            for c in range(2):
                last = nc.tensor.matmul(psD[0][:, c:c + 1], carry[0:1, c * P:(c + 1) * P], ones_f[0:1, 0:1],
                                        start=True, stop=True)
            last.then_inc(carry_in, 1)
            pe.wait_ge(deg_ready, 1)
            pe.wait_ge(w_in, 2 * 7 * 16)
            pe.wait_ge(idx_ready, 1)
            for t in range(2):
                for c in range(2):
                    for o, g in enumerate((2, 0, 1)):
                        nc.tensor.transpose((psS if c == 0 else psD)[t][:, o * P:(o + 1) * P],
                                            wih_sb[t][:, g, c * P:(c + 1) * P], ident[:, :])
                for g in range(3):
                    last = nc.tensor.transpose(psG[t][:, 0, g * P:(g + 1) * P], whh_sb[t][:, g, :], ident[:, :])
            last.then_inc(w_t, 1)
            pe.wait_ge(w_tc, 1)
            pe.wait_ge(bm_ready, 1)
            for t in range(2):
                for c in range(2):
                    nc.tensor.matmul(psS[t][:, 0:3 * P], wmsg_sb[t][:, c, 0:P], wihT[t][:, c, :],
                                     start=(c == 0), stop=(c == 1))
                for c in range(2):
                    nc.tensor.matmul(psD[t][:, 0:3 * P], wmsg_sb[t][:, c, P:2 * P], wihT[t][:, c, :],
                                     start=(c == 0), stop=(c == 1))
                for c in range(2):
                    last = nc.tensor.matmul(psG[t][0:96, 1, 0:3 * P], bm_rep[t][:, c, :], wihT[t][:, c, :],
                                            start=(c == 0), stop=(c == 1))
            last.then_inc(w_c, 1)
            pe.wait_ge(w_ready, 1)

            def turn(R, b, u, i, dst_n):
                k, v = u % RING, u % 2
                pe.wait_ge(R.src_in[k], (uses(u, i) + 1) * 16 * TILES)
                pe.wait_ge(R.dst_in[k], (uses(u, i) + 1) * dst_n)
                if at_least(b, 2):
                    pe.wait_ge(R.scanned, b - 1)
                for t in range(TILES):
                    nc.tensor.transpose(psS[v][:, t * P:(t + 1) * P], srcbuf[k][:, t * P:(t + 1) * P], ident[:, :])
                for t in range(TILES):
                    last = nc.tensor.transpose(psD[v][:, t * P:(t + 1) * P], dstbuf[k][:, t * P:(t + 1) * P],
                                               ident[:, :])
                last.then_inc(R.turned, 1)

            def gates(R, w, b, u, i):
                v = u % 2
                pe.wait_ge(R.scanned, b + 1)
                pe.wait_ge(R.hT_ready, b + 1)
                pe.wait_ge(R.rows_in[u % RING], (uses(u, i) + 1) * (48 if R is R1 else 64))
                for g in range(2):
                    q = 2 * b + g
                    if at_least(b, 1):
                        pe.wait_ge(R.npre_done, q - 1)
                    for t in range(2):
                        c = slice((2 * g + t) * P, (2 * g + t + 1) * P)
                        G = psG[g][:, t, :]
                        nc.tensor.matmul(G, degl[u % RING][:, c], WB[w][:, :], start=True, stop=False)
                        nc.tensor.matmul(G[:, 0:3 * P], aT[v][:, c], WA[w][:, :], start=False, stop=False)
                        nc.tensor.matmul(G[:, 0:3 * P], dhT[v][:, c], WD[w][:, :], start=False, stop=False)
                        last = nc.tensor.matmul(G[:, P:4 * P], hT[v][:, c], WH[w][:, :], start=False, stop=True)
                    last.then_inc(R.gated, 1)

            for R, w, dst_n in ((R1, 0, 16 * TILES), (R2, 1, 1)):
                def step(b, u, i):
                    if not known(b) or b < LAST:
                        turn(R, b + 1, (u + 1) % WIDE, i + (u == WIDE - 1), dst_n)
                    gates(R, w, b, u, i)

                turn(R, 0, 0, 0, dst_n)
                bodies(pe, step)
                step(LAST, 0, BODIES)

        @block.scalar
        def _(act):
            act.wait_ge(w_t, 1)
            for t in range(2):
                nc.scalar.activation(wihT[t][:, 0, :], psS[t][:, 0:3 * P], ACT.Copy)
                nc.scalar.activation(wihT[t][:, 1, :], psD[t][:, 0:3 * P], ACT.Copy)
                last = nc.scalar.activation(WH[t][:, :], psG[t][:, 0, 0:3 * P], ACT.Copy)
            last.then_inc(w_tc, 1)

            def evac(R, b, u):
                act.wait_ge(R.turned, b + 1)
                if at_least(b, 2):
                    act.wait_ge(R.gated, 2 * (b - 1))
                nc.scalar.activation(hT[u % 2][:, :], psD[u % 2][:, :], ACT.Copy).then_inc(R.hT_ready, 1)

            def sigmoids(R, b, g):
                q = 2 * b + g
                act.wait_ge(R.gated, q + 1)
                if at_least(b, 1):
                    act.wait_ge(R.updated, q - 1)
                nc.scalar.activation(rz[g][:, :, :], psG[g][:, :, P:3 * P], ACT.Sigmoid).then_inc(R.rz_ready, 1)

            def tanhs(R, b, g):
                act.wait_ge(R.npre_done, 2 * b + g + 1)
                nc.scalar.activation(nn[g][:, :, :], npre[g][:, :, :], ACT.Tanh).then_inc(R.tanh_done, 1)

            def ln_sqrt(s, v):
                act.wait_ge(ln_w, s + 1)
                nc.scalar.activation(small[v][0:ln_p(s), 4, :], small[v][0:ln_p(s), 3, :], ACT.Sqrt,
                                     bias=eps_col[0:ln_p(s), :]).then_inc(ln_sd, 1)

            def ln_apply(s, k, piece=None):
                act.wait_ge(ln_coef, s + 1)
                n, v = ln_p(s), k % 2
                rows = range(LN_ROWS) if piece is None else range(4 * piece, 4 * piece + 4)
                for r in rows:
                    last = nc.scalar.activation(lnbuf[k][0:n, r, :], lnbuf[k][0:n, r, :], ACT.Identity,
                                                bias=small[v][0:n, 7, r:r + 1], scale=small[v][0:n, 6, r:r + 1])
                if piece in (None, 3):
                    last.then_inc(ln_done, 1)

            def step(b, u, i):
                for g in range(2):
                    w = 2 * u + g
                    if g == 1:
                        tanhs(R1, b, 0)
                    elif at_least(b, 1):
                        tanhs(R1, b - 1, 1)
                    if g == 0 and (not known(b) or b < LAST):
                        evac(R1, b + 1, u + 1)
                    if at_least(b, 2) and w % 4 == 0:
                        ln_sqrt(4 * i + w // 4 - 1, (w // 4 - 1) % 2)
                    if at_least(b, 3) and not (known(b) and 2 * b + g < APPLY_LAG):
                        a = w - APPLY_LAG
                        ln_apply(4 * i + a // 4, (a // 4) % 4, a % 4)
                    sigmoids(R1, b, g)

            evac(R1, 0, 0)
            bodies(act, step)
            step(LAST, 0, BODIES)
            tanhs(R1, LAST, 1)
            for a in range(2 * NB - APPLY_LAG, 4 * LN_1A):
                ln_apply(a // 4, (a // 4) % 4, a % 4)

            def stage_h1(b, u, i):
                k = u % RING
                act.wait_ge(R1.updated, 2 * b + 2)
                if at_least(b, RING):
                    act.wait_ge(scattered[k], uses(u, i) * 16 * TILES)
                else:
                    act.wait_ge(R1.turned, NB)
                nc.scalar.activation(srcbuf[k][:, :], h1[:, cols(b)], ACT.Copy).then_inc(h1_staged, 1)

            def step_b(s, k, before):
                j = before - BODIES
                for u in (2 * k, 2 * k + 1):
                    stage_h1(j * WIDE + u, u, j)
                ln_sqrt(s, k % 2)
                if at_least(s, LN_1A + 1):
                    ln_apply(s - 1, (k - 1) % 4)

            ln_bodies(act, step_b)
            stage_h1(LAST, 0, BODIES)
            ln_sqrt(LN_FULL, 0)
            ln_apply(LN_FULL - 1, 3)
            ln_apply(LN_FULL, 0)

            def load_h(b, u):
                if at_least(b, RING):
                    act.wait_ge(R2.updated, 2 * (b - RING) + 2)
                nc.scalar.activation(dstbuf[u % RING][:, :], h1[:, cols(b)], ACT.Copy)\
                  .then_inc(R2.dst_in[u % RING], 1)

            def f_sqrt(b, v):
                act.wait_ge(f_w, b + 1)
                nc.scalar.activation(small[v][:, 4, 0:TILES], small[v][:, 3, 0:TILES], ACT.Sqrt,
                                     bias=eps_col[:, :], scale=0.25).then_inc(f_sd, 1)

            def f_apply(b, u):
                act.wait_ge(f_coef, b + 1)
                y, v = y_rows(u), u % 2
                for t in range(TILES):
                    last = nc.scalar.activation(y[:, t, :], y[:, t, :], ACT.Identity,
                                                bias=small[v][:, 7, t:t + 1], scale=small[v][:, 5, t:t + 1])
                last.then_inc(f_done, 1)

            for u in range(RING):
                act.wait_ge(spilled[u], (uses(0, BODIES) + (u == 0)) * 16)
            for u in range(RING - 1):
                load_h(u, u)
            evac(R2, 0, 0)

            def step_2(b, u, i):
                if at_least(b, 1):
                    tanhs(R2, b - 1, 1)
                if not known(b) or b < LAST:
                    evac(R2, b + 1, u + 1)
                if at_least(b, 2):
                    f_apply(b - 2, (u - 2) % WIDE)
                sigmoids(R2, b, 0)
                tanhs(R2, b, 0)
                if not known(b) or b + RING - 2 <= LAST and b >= 1:
                    load_h(b + RING - 2, u + RING - 2)
                if at_least(b, 1):
                    f_sqrt(b - 1, (u - 1) % 2)
                sigmoids(R2, b, 1)

            bodies(act, step_2)
            step_2(LAST, 0, BODIES)
            tanhs(R2, LAST, 1)
            f_apply(LAST - 1, (LAST - 1) % WIDE)
            f_sqrt(LAST, 0)
            f_apply(LAST, 0)

        @block.vector
        def _(dve):
            links = [0]

            def link(ins):
                links[0] += 1
                ins.then_inc(prep_v, 1)
                dve.wait_ge(prep_v, links[0])

            for k in range(RING):
                nc.vector.memset(degl[k][0:64, :], 0.0)
                nc.vector.memset(degl[k][64:96, :], 1.0)
            last = nc.vector.memset(ones_f, 1.0)
            for k in range(2):
                nc.vector.memset(aT[k][:, SLOTS - 1:SLOTS], 0.0)
                nc.vector.memset(dhT[k][:, SLOTS - 1:SLOTS], 0.0)
            nc.vector.memset(carry[0:1, 0:1], 0.0)
            for k in range(4):
                nc.vector.memset(f_idx[k], 0.0)
            nc.vector.memset(f_same, 0.0)
            link(nc.vector.memset(f_out, 0.0))
            dve.wait_ge(idx_in, 8 * 16)
            for k in range(4):
                nc.vector.tensor_copy(f_idx[k][:, 0:P], raw_idx[k][:, 0:P])
                last = nc.vector.tensor_copy(f_idx[k][0:NT - P, P:2 * P], raw_idx[k][0:NT - P, P:2 * P])
            link(last)
            link(nc.vector.tensor_tensor(f_same, f_idx[0], f_idx[1], ALU.is_equal))
            nc.vector.tensor_tensor(f_prev, f_idx[0], f_idx[3], ALU.is_equal)
            for c in range(2):
                h = slice(c * P, (c + 1) * P)
                nc.vector.tensor_scalar(f_head[:, h], f_idx[0][:, h], f_idx[3][:, c * P:c * P + 1], None,
                                        ALU.is_equal)
            link(nc.vector.tensor_scalar(f_node, f_idx[0], 0.0, None, ALU.max))
            nc.vector.scalar_tensor_tensor(out=f_out, in0=f_same, scalar=SKIP, in1=f_node,
                                           op0=ALU.mult, op1=ALU.add).then_inc(idx_f, 1)
            dve.wait_ge(idx_t, 1)
            for k in range(3):
                last = nc.vector.tensor_copy(
                    idx_all[:, :, k, :], psG[k % 2][:, k // 2, 0:NT].rearrange("p (b t) -> p b t", t=TILES))
            link(last)

            def stage_idx(b, u, ready, scat=False):
                d, a = (stage_out, slice(2, 3)) if scat else (stage, slice(0, 2))
                nc.vector.tensor_copy(d[u][:, :].rearrange("p (b k t) -> p b k t", b=1, t=TILES),
                                      idx_all[:, bass.ds(b, 1), a, :]).then_inc(ready, 1)

            for u in range(RING):
                stage_idx(u, u, staged)
            for c in range(2):
                h = slice(c * P, (c + 1) * P)
                last = nc.vector.tensor_tensor_scan(f_local[:, h], f_prev[:, h], ones_f[:, h], 0.0,
                                                    ALU.mult, ALU.add)
            last.then_inc(ends_ready, 1)
            dve.wait_ge(consts, 3)
            link(nc.vector.tensor_tensor(sel[:, :], ident[:, 0:3], ident[:, 32:35], ALU.add))
            nc.vector.tensor_tensor(sel[:, :], sel[:, :], ident[:, 64:67], ALU.add).then_inc(idx_ready, 1)

            dve.wait_ge(ends_row, 1)
            link(nc.vector.tensor_copy(ends[0:1, :], psS[0][0:1, :]))
            nc.vector.tensor_tensor_scan(carry[0:1, 1:2 * P + 1], ends[0:1, 2 * P:4 * P], ends[0:1, 0:2 * P], 0.0,
                                         ALU.mult, ALU.add).then_inc(carry_row, 1)
            dve.wait_ge(carry_in, 1)
            link(nc.vector.tensor_copy(carry_col, psD[0][:, 0:2]))
            for c in range(2):
                h = slice(c * P, (c + 1) * P)
                last = nc.vector.scalar_tensor_tensor(out=f_deg[:, h], in0=f_head[:, h], scalar=carry_col[:, c:c + 1],
                                                      in1=f_local[:, h], op0=ALU.mult, op1=ALU.add)
            link(last)
            nc.vector.tensor_copy(b_same, f_prev)
            link(nc.vector.tensor_copy(b_hi, f_deg))
            nc.vector.tensor_tensor(b_lo, f_deg, b_hi, ALU.subtract).then_inc(deg_ready, 1)

            dve.wait_ge(w_in, 2 * 7 * 16)
            for t in range(2):
                for c in range(2):
                    last = nc.vector.tensor_copy(bm_rep[t][:, c, :], bm_col[t][:, c:c + 1].broadcast_to([P, 96]))
            last.then_inc(bm_ready, 1)
            dve.wait_ge(w_tc, 1)
            dve.wait_ge(idx_ready, 1)
            dve.wait_ge(w_c, 1)
            for t in range(2):
                nc.vector.tensor_copy(WA[t][:, :], psS[t][:, 0:3 * P])
                nc.vector.tensor_copy(WD[t][:, :], psD[t][:, 0:3 * P])
                B, bi, bh = bias_f[t], bih_rep[t], bhh_rep[t]
                nc.vector.tensor_copy(B[0:64, 0:3 * P], psG[t][0:64, 1, 0:3 * P])
                nc.vector.memset(B[0:64, 3 * P:4 * P], 0.0)
                nc.vector.tensor_copy(B[64:96, 0:P], bi[64:96, 2 * P:3 * P])
                nc.vector.tensor_tensor(B[64:96, P:3 * P], bi[64:96, 0:2 * P], bh[64:96, 0:2 * P], ALU.add)
                link(nc.vector.tensor_copy(B[64:96, 3 * P:4 * P], bh[64:96, 2 * P:3 * P]))
                rem = B
                for k in range(3):
                    link(nc.vector.tensor_copy(part[t][k][0:96, :], rem[0:96, :]))
                    if k < 2:
                        link(nc.vector.tensor_tensor(rest[t][k][0:96, :], rem[0:96, :], part[t][k][0:96, :],
                                                     ALU.subtract))
                        rem = rest[t][k]
                link(nc.vector.tensor_scalar(pick[t][0][0:96, :], part[t][0][0:96, :], sel[0:96, 0:1], None, ALU.mult))
                link(nc.vector.scalar_tensor_tensor(out=pick[t][1][0:96, :], in0=part[t][1][0:96, :],
                                                    scalar=sel[0:96, 1:2], in1=pick[t][0][0:96, :],
                                                    op0=ALU.mult, op1=ALU.add))
                last = nc.vector.scalar_tensor_tensor(out=WB[t][:, :], in0=part[t][2][0:96, :],
                                                      scalar=sel[0:96, 2:3], in1=pick[t][1][0:96, :],
                                                      op0=ALU.mult, op1=ALU.add)
            last.then_inc(w_ready, 1)

            def scan_src(R, b, u, i):
                v = u % 2
                dve.wait_ge(R.rows_in[u % RING], (uses(u, i) + 1) * (48 if R is R1 else 64))
                dve.wait_ge(R.turned, b + 1)
                if at_least(b, 2):
                    dve.wait_ge(R.gated, 2 * (b - 1))
                if at_least(b, 1):
                    dve.wait_ge(R.scan_a, b)
                nc.vector.tensor_tensor_scan(aT[v][:, :], same[u % RING][:, :], psS[v][:, :],
                                             aT[1 - v][:, SLOTS - 1:SLOTS], ALU.mult, ALU.add).then_inc(R.scan_a, 1)

            def scan_dst(R, b, u):
                v = u % 2
                dve.wait_ge(R.hT_ready, b + 1)
                if R is R1:
                    if at_least(b, 1):
                        dve.wait_ge(R.scanned, b)
                    nc.vector.tensor_tensor_scan(dhT[v][:, :], same[u % RING][:, :], psD[v][:, :],
                                                 dhT[1 - v][:, SLOTS - 1:SLOTS], ALU.mult, ALU.add)\
                      .then_inc(R.scanned, 1)
                else:
                    nc.vector.tensor_tensor(dhT[v][:, :], deg_rep[u % RING], psD[v][:, :], ALU.mult)\
                      .then_inc(R.scanned, 1)

            def candidate(R, b, g):
                dve.wait_ge(R.rz_ready, 2 * b + g + 1)
                nc.vector.tensor_tensor(npre[g][:, :, :], rz[g][:, :, 0:P], psG[g][:, :, 3 * P:4 * P],
                                        ALU.mult).then_inc(R.rh_done, 1)
                dve.wait_ge(R.rh_done, 2 * b + g + 1)
                nc.vector.tensor_tensor(npre[g][:, :, :], npre[g][:, :, :], psG[g][:, :, 0:P],
                                        ALU.add).then_inc(R.npre_done, 1)

            def update(R, b, u, g, to, between=(None, None)):
                h = dstbuf[u % RING][:, g * 2 * P:(g + 1) * 2 * P].rearrange("p (t f) -> p t f", t=2)
                dve.wait_ge(R.tanh_done, 2 * b + g + 1)
                nc.vector.tensor_tensor(dd[g][:, :, :], h, nn[g][:, :, :], ALU.subtract).then_inc(R.diff_done, 1)
                if between[0]:
                    between[0]()
                dve.wait_ge(R.diff_done, 2 * b + g + 1)
                nc.vector.tensor_tensor(dd[g][:, :, :], rz[g][:, :, P:2 * P], dd[g][:, :, :], ALU.mult)\
                  .then_inc(R.zd_done, 1)
                if between[1]:
                    between[1]()
                dve.wait_ge(R.zd_done, 2 * b + g + 1)
                nc.vector.tensor_tensor(to, nn[g][:, :, :], dd[g][:, :, :], ALU.add).then_inc(R.updated, 1)

            def h1_group(b, g):
                return h1[:, bass.ds(b * SLOTS + g * 2 * P, 2 * P)].rearrange("p (t f) -> p t f", t=2)

            def moments(v, n, rows, bn, total, w):
                S, T = small[v], st[v]
                dve.wait_ge(bn[0], bn[1])
                nc.vector.tensor_tensor(S[0:n, 0, 0:rows], T[0:n, 0:rows, 1], T[0:n, 0:rows, 4], ALU.add)
                nc.vector.tensor_tensor(S[0:n, 1, 0:rows], T[0:n, 0:rows, 1], T[0:n, 0:rows, 4], ALU.subtract)
                nc.vector.tensor_tensor(S[0:n, 2, 0:rows], T[0:n, 0:rows, 2], T[0:n, 0:rows, 5], ALU.add)\
                  .then_inc(total[0], 1)
                dve.wait_ge(total[0], 2 * total[1] - 1)
                nc.vector.tensor_tensor(S[0:n, 1, 0:rows], S[0:n, 1, 0:rows], S[0:n, 1, 0:rows], ALU.mult)\
                  .then_inc(total[0], 1)
                dve.wait_ge(total[0], 2 * total[1])
                nc.vector.scalar_tensor_tensor(out=S[0:n, 3, 0:rows], in0=S[0:n, 2, 0:rows], scalar=4.0 / P,
                                               in1=S[0:n, 1, 0:rows], op0=ALU.mult, op1=ALU.add).then_inc(w, 1)

            def ln_stats(s, k, rows):
                n, v = ln_p(s), k % 2
                for r in rows:
                    last = nc.vector.bn_stats(st[v][0:n, r, :], lnbuf[k][0:n, r, :])
                if rows[-1] == LN_ROWS - 1:
                    last.then_inc(ln_bn, 1)

            def ln_begin(s, k, before):
                dve.wait_ge(ln_in[k], before * 16 + 16)

            def ln_moments(s, k):
                if at_least(s, 2):
                    dve.wait_ge(ln_done, s - 1)
                moments(k % 2, ln_p(s), LN_ROWS, (ln_bn, s + 1), (ln_sum, s + 1), ln_w)

            def ln_finish(s, v):
                n, S = ln_p(s), small[v]
                dve.wait_ge(ln_sd, s + 1)
                nc.vector.reciprocal(S[0:n, 5, :], S[0:n, 4, :]).then_inc(ln_rs, 1)
                dve.wait_ge(ln_rs, s + 1)
                nc.vector.tensor_scalar(S[0:n, 6, :], S[0:n, 5, :], 2.0, None, ALU.mult)
                nc.vector.scalar_tensor_tensor(out=S[0:n, 7, :], in0=S[0:n, 0, :], scalar=-1.0, in1=S[0:n, 5, :],
                                               op0=ALU.mult, op1=ALU.mult).then_inc(ln_coef, 1)

            def step(b, u, i):
                if not known(b) or b + RING <= LAST:
                    dve.wait_ge(R1.src_in[u % RING], (uses(u, i) + 1) * 16 * TILES)
                    dve.wait_ge(R1.dst_in[u % RING], (uses(u, i) + 1) * 16 * TILES)
                    stage_idx(b + RING, u % RING, staged)
                for g in range(2):
                    w = 2 * u + g
                    more = not known(b) or b < LAST
                    if g == 0 and more:
                        scan_src(R1, b + 1, u + 1 if u + 1 < WIDE else 0, i + (u + 1 == WIDE))
                    if g == 1 and more:
                        scan_dst(R1, b + 1, u + 1)
                    s, k, r = 4 * i + w // 4, (w // 4) % 4, 4 * (w % 4)
                    if more and w % 4 == 0:
                        ln_begin(s, k, i)
                    fill = (lambda: ln_stats(s, k, range(r, r + 2)), lambda: ln_stats(s, k, range(r + 2, r + 4)))
                    fill = fill if more else (None, None)
                    if g == 1:
                        update(R1, b, u, 0, h1_group(b, 0), fill)
                    elif at_least(b, 1):
                        update(R1, b - 1, u - 1, 1, h1_group(b - 1, 1), fill)
                    else:
                        fill[0]()
                        fill[1]()
                    if more and w % 4 == 3:
                        ln_moments(s, k)
                    if w % 4 == 1 and at_least(b, 2):
                        ln_finish(4 * i + w // 4 - 1, (w // 4 - 1) % 2)
                    candidate(R1, b, g)

            dve.wait_ge(w_ready, 1)
            scan_src(R1, 0, 0, 0)
            scan_dst(R1, 0, 0)
            bodies(dve, step)
            step(LAST, 0, BODIES)
            update(R1, LAST, 0, 1, h1_group(LAST, 1))

            def stage_sct(b, u, i):
                if at_least(b, RING):
                    dve.wait_ge(scattered[u % RING], uses(u, i) * 16 * TILES)
                stage_idx(b, u % RING, sct_staged, scat=True)

            def step_b(s, k, before):
                j = before - BODIES
                for u in (2 * k, 2 * k + 1):
                    stage_sct(j * WIDE + u, u, j)
                ln_begin(s, k, before)
                ln_stats(s, k, range(LN_ROWS))
                ln_moments(s, k)
                if at_least(s, LN_1A + 1):
                    ln_finish(s - 1, (k - 1) % 2)

            ln_bodies(dve, step_b)
            stage_sct(LAST, 0, BODIES)
            ln_begin(LN_FULL, 0, BODIES + LN_BODIES)
            ln_stats(LN_FULL, 0, range(LN_ROWS))
            ln_moments(LN_FULL, 0)
            ln_finish(LN_FULL - 1, 1)
            ln_finish(LN_FULL, 0)

            for u in range(RING):
                stage_idx(u, u, staged2)
            dve.wait_ge(R1.scanned, NB)
            for k in range(2):
                last = nc.vector.memset(aT[k][:, SLOTS - 1:SLOTS], 0.0)
            link(last)
            for u in range(RING):
                dve.wait_ge(scattered[u], (uses(0, BODIES) + (u == 0)) * 16 * TILES)
            dve.wait_ge(ln_done, LN_FULL + 1)

            def residual(b, u, i, g):
                y, k = y_rows(u), u % RING
                if g == 0:
                    dve.wait_ge(xd_in[k], uses(u, i) * 16 + 16)
                    if not known(i) or i > 0:
                        dve.wait_ge(final_out[u], i * 16 * TILES)
                dve.wait_ge(R2.updated, 2 * b + g + 1)
                nc.vector.tensor_tensor(y[:, 2 * g:2 * g + 2, :], hout[g][:, :, :],
                                        lnbuf[2][:, TILES * k + 2 * g:TILES * k + 2 * g + 2, :], ALU.add)\
                  .then_inc(y_done, 1)

            def y_stats(b, u, g):
                dve.wait_ge(y_done, 2 * b + g + 1)
                for t in (2 * g, 2 * g + 1):
                    last = nc.vector.bn_stats(st[u % 2][:, t, :], y_rows(u)[:, t, :])
                if g == 1:
                    last.then_inc(f_bn, 1)
                    if at_least(b, 2):
                        dve.wait_ge(f_done, b - 1)
                    moments(u % 2, P, TILES, (f_bn, b + 1), (f_sum, b + 1), f_w)

            def finish(b, v):
                S = small[v]
                dve.wait_ge(f_sd, b + 1)
                nc.vector.reciprocal(S[:, 5, 0:TILES], S[:, 4, 0:TILES]).then_inc(f_rs, 1)
                dve.wait_ge(f_rs, b + 1)
                nc.vector.scalar_tensor_tensor(out=S[:, 7, 0:TILES], in0=S[:, 0, 0:TILES], scalar=-0.5,
                                               in1=S[:, 5, 0:TILES], op0=ALU.mult, op1=ALU.mult).then_inc(f_coef, 1)

            def step_2(b, u, i):
                more = not known(b) or b < LAST
                if not known(b) or b + RING <= LAST:
                    dve.wait_ge(R2.src_in[u % RING], (uses(u, i) + 1) * 16 * TILES)
                    stage_idx(b + RING, u % RING, staged2)
                if not known(i) or i > 0:
                    dve.wait_ge(final_out[u], i * 16 * TILES)
                stage_idx(b, u, out_staged, scat=True)
                if more:
                    scan_src(R2, b + 1, u + 1 if u + 1 < WIDE else 0, i + (u + 1 == WIDE))
                if at_least(b, 1):
                    pu, pi = (u - 1) % WIDE, i - (u == 0)
                    update(R2, b - 1, pu, 1, hout[1][:, :, :])
                    residual(b - 1, pu, pi, 1)
                    y_stats(b - 1, pu, 1)
                candidate(R2, b, 0)
                if more:
                    scan_dst(R2, b + 1, u + 1)
                update(R2, b, u, 0, hout[0][:, :, :])
                residual(b, u, i, 0)
                y_stats(b, u, 0)
                if at_least(b, 1):
                    finish(b - 1, (u - 1) % 2)
                candidate(R2, b, 1)

            scan_src(R2, 0, 0, 0)
            scan_dst(R2, 0, 0)
            bodies(dve, step_2)
            step_2(LAST, 0, BODIES)
            update(R2, LAST, 0, 1, hout[1][:, :, :])
            residual(LAST, 0, BODIES, 1)
            y_stats(LAST, 0, 1)
            finish(LAST, 0)


_INS = ["x", "src", "dst", "L0_gnn_W_msg", "L0_gnn_b_msg", "L0_gnn_W_ih", "L0_gnn_W_hh", "L0_gnn_b_ih", "L0_gnn_b_hh"]


def kernel(**inputs):
    import numpy as np
    import concourse.bacc as bacc
    from concourse import mybir as mb
    from concourse.bass_utils import run_bass_kernel_spmd as run

    nc = bacc.Bacc("TRN2", target_bir_lowering=False, num_devices=1)
    arrays, args = {}, []
    for name in _INS:
        a = np.ascontiguousarray(inputs[name])
        arrays[f"in_{name}"] = a
        args.append(nc.dram_tensor(f"in_{name}", a.shape, mb.dt.from_np(a.dtype), kind="ExternalInput").ap())
    out = nc.dram_tensor("out_rows", arrays["in_x"].shape, mb.dt.float32, kind="ExternalOutput").ap()
    build(nc, *args, out)
    r = run(nc, [arrays], core_ids=[0])
    return r.results[0]["out_rows"]
```

```python
from contextlib import ExitStack

import concourse.bass as bass
from concourse import mybir

P = 128
TILES = 4
SLOTS = P * TILES
RING = 4
WIDE = 8
LAG = 5
SCT_LAG = 2
LN_ROWS = 16
ACT_ROWS = 14
SKIP = float(1 << 20)
EPS = 1e-5

F32 = mybir.dt.float32
BF16 = mybir.dt.bfloat16
F32R = mybir.dt.float32r
I32 = mybir.dt.int32
ALU = mybir.AluOpType
ACT = mybir.ActivationFunctionType


def build(nc, x, src, dst, W_msg, b_msg, W_ih, W_hh, b_ih, b_hh, out):
    N, H = x.shape
    E = src.shape[0]
    assert H == P and W_msg.shape[0] == 2
    NB = -(-E // SLOTS)
    NT = NB * TILES
    EP = NB * SLOTS
    LAST = NB - 1
    BODIES1 = LAST // RING
    BODIES = LAST // WIDE
    assert NB == BODIES1 * RING + 1 == BODIES * WIDE + 1
    HALF = BODIES1 // 2
    FIRST_B = HALF * RING
    assert HALF >= 2 and BODIES1 - HALF >= 3 and SCT_LAG <= RING
    LN_FULL = N // (P * LN_ROWS)
    LN_TAIL_P = (N - LN_FULL * P * LN_ROWS) // LN_ROWS
    assert LN_TAIL_P * LN_ROWS + LN_FULL * P * LN_ROWS == N and 0 < LN_TAIL_P < P
    assert LN_FULL == 2 * (LAST - FIRST_B) == LAST
    PREP_CHUNKS = 2
    CHUNKS = PREP_CHUNKS + 2 * FIRST_B + RING
    COPY = N // (CHUNKS * 16) * 16
    COPY_REST = N - COPY * CHUNKS
    assert 0 < COPY_REST < COPY and COPY_REST % 16 == 0 and CHUNKS % 2 == 0 and PREP_CHUNKS == 2
    LN_STEPS = 14
    assert LN_STEPS < LN_ROWS
    GUESS = float(0x5f3759df - (1 << 30) - (1 << 22))
    PAIRS_UP_TO = 2 * (LAST - 2 - FIRST_B) + 1
    assert PAIRS_UP_TO == LAST - 3
    GATES = 4 * P

    ctx = ExitStack()
    with ctx:
        def sb(name, shape, dt=F32):
            return ctx.enter_context(nc.sbuf_tensor(name, shape, dt))

        def sem(name):
            return ctx.enter_context(nc.semaphore(name))

        def sems(name, n):
            return [sem(f"{name}{k}") for k in range(n)]

        dst_s = nc.dram_tensor("dst_s", [EP + 2], I32, kind="Internal").ap()
        src_s = nc.dram_tensor("src_s", [EP], I32, kind="Internal").ap()
        h_table = nc.dram_tensor("h_table", [N, P], F32, kind="Internal").ap()
        xd_spill = nc.dram_tensor("xd_spill", [NB, P, SLOTS], F32, kind="Internal").ap()
        rows_d = nc.dram_tensor("rows_d", [3, EP], BF16, kind="Internal").ap()

        deg_d = nc.dram_tensor("deg_d", [1, EP], F32, kind="Internal").ap()

        h1 = sb("h1", [P, EP])
        srcbuf = [sb(f"srcbuf{k}", [P, SLOTS]) for k in range(RING)]
        dstbuf = [sb(f"dstbuf{k}", [P, SLOTS]) for k in range(RING)]
        aT = [sb(f"aT{k}", [P, SLOTS]) for k in range(2)]
        dhT = [sb(f"dhT{k}", [P, SLOTS]) for k in range(2)]
        rz = [sb(f"rz{k}", [P, 2, 2 * P]) for k in range(2)]
        npre = [sb(f"npre{k}", [P, 2, P]) for k in range(2)]
        nn = [sb(f"nn{k}", [P, 2, P]) for k in range(2)]
        dd = [sb(f"dd{k}", [P, 2, P]) for k in range(2)]
        same = [sb(f"same{k}", [P, SLOTS], BF16) for k in range(RING)]
        degl = [sb(f"degl{k}", [96, SLOTS], BF16) for k in range(RING)]
        idx_all = sb("idx_all", [P, NB, 3, TILES], I32)
        stage = [sb(f"stage{k}", [P, 2 * TILES], I32) for k in range(RING)]
        stage_out = [sb(f"stage_out{k}", [P, TILES], I32) for k in range(WIDE)]
        WA = [sb("WA0", [P, 3 * P]), sb("WA1", [P, 3 * P], F32R)]
        WA_lo = sb("WA_lo", [P, 3 * P], F32R)
        WD = [sb(f"WD{t}", [P, 3 * P]) for t in range(2)]
        WH = [sb("WH0", [P, 3 * P]), sb("WH1", [P, 3 * P], F32R)]
        WH1_lo = sb("WH1_lo", [P, 3 * P], F32R)
        WB = [sb(f"WB{t}", [96, GATES], BF16) for t in range(2)]
        ident = sb("ident", [P, P])
        sel = sb("sel", [P, 3])
        eps_col = sb("eps_col", [P, 1])
        st = [sb(f"st{k}", [P, LN_ROWS, 6]) for k in range(2)]
        small = [sb(f"small{k}", [P, 8, LN_ROWS]) for k in range(2)]

        psS = [ctx.enter_context(nc.psum_tensor(f"psS{k}", [P, SLOTS], F32)) for k in range(2)]
        psD = [ctx.enter_context(nc.psum_tensor(f"psD{k}", [P, SLOTS], F32)) for k in range(2)]
        psG = [ctx.enter_context(nc.psum_tensor(f"psG{k}", [P, 2, GATES], F32)) for k in range(2)]

        with ExitStack() as first:
            def sb_1(name, shape):
                return first.enter_context(nc.sbuf_tensor(name, shape, F32))

            hT = [sb_1(f"hT{k}", [P, SLOTS]) for k in range(2)]
            sctbuf = [sb_1(f"sctbuf{k}", [P, SLOTS]) for k in range(RING)]
            lnbuf = [sb_1(f"lnbuf{k}", [P, LN_ROWS, P]) for k in (1, 2, 3, 0)]
            lnbuf = lnbuf[3:] + lnbuf[:3]
        hT_hi = [sb(f"hT_hi{k}", [P, SLOTS], F32R) for k in range(2)]
        hT_lo = [sb(f"hT_lo{k}", [P, SLOTS], F32R) for k in range(2)]
        with ExitStack() as phase_1a:
            WH0_parts = [phase_1a.enter_context(nc.sbuf_tensor(f"WH0_{n}", [P, 3 * P], F32R)) for n in ("hi", "lo")]
        aT_hi = [sb(f"aT_hi{k}", [P, SLOTS], F32R) for k in range(2)]
        aT_lo = [sb(f"aT_lo{k}", [P, SLOTS], F32R) for k in range(2)]
        deg_rep = [sb(f"deg_rep{k}", [P, SLOTS]) for k in range(RING)]
        xd = [sb(f"xd{k}", [P, TILES, P]) for k in range(RING)]
        y = [sb(f"y{k}", [P, TILES, P]) for k in range(WIDE)]
        hout = npre
        WH_parts = [WH0_parts, (WH[1], WH1_lo)]

        off = [0]

        def over_h1(cols, dt=F32):
            a = h1[:, off[0]:off[0] + cols]
            off[0] += cols
            return a if dt is F32 else a.bitcast(dt)

        raw_idx = [over_h1(2 * P, I32) for _ in range(4)]
        f_idx = [over_h1(2 * P) for _ in range(4)]
        f_same = over_h1(2 * P)
        f_out = over_h1(2 * P)
        f_node, f_prev, f_head, f_local, f_deg = (over_h1(2 * P) for _ in range(5))
        ones_f = over_h1(2 * P)
        pad_idx = over_h1(2 * P, I32)[0:1, :]
        ends = over_h1(4 * P)
        carry = over_h1(2 * P + 2)
        carry_col = over_h1(2)
        b_same, b_hi, b_lo = (over_h1(P, BF16) for _ in range(3))
        wmsg_sb = [over_h1(2 * 2 * P).rearrange("p (c f) -> p c f", c=2) for _ in range(2)]
        wih_sb = [over_h1(3 * 2 * P).rearrange("p (g f) -> p g f", g=3) for _ in range(2)]
        whh_sb = [over_h1(3 * P).rearrange("p (g f) -> p g f", g=3) for _ in range(2)]
        wihT = [over_h1(2 * 3 * P).rearrange("p (c g) -> p c g", c=2) for _ in range(2)]
        bm_col = [over_h1(2) for _ in range(2)]
        bm_rep = [over_h1(2 * 96).rearrange("p (c r) -> p c r", c=2) for _ in range(2)]
        bih_rep = [over_h1(3 * P) for _ in range(2)]
        bhh_rep = [over_h1(3 * P) for _ in range(2)]
        bias_f = [over_h1(GATES) for _ in range(2)]
        part = [[over_h1(GATES // 2, BF16) for _ in range(3)] for _ in range(2)]
        rest = [[over_h1(GATES) for _ in range(2)] for _ in range(2)]
        pick = [[over_h1(GATES) for _ in range(3)] for _ in range(2)]
        assert off[0] <= EP

        pad_set = sem("pad_set")
        lists_in = sem("lists_in")
        idx_in = sem("idx_in")
        w_in = sem("w_in")
        consts = sem("consts")
        prep_v = sem("prep_v")
        idx_f = sem("idx_f")
        idx_t = sem("idx_t")
        idx_ready = sem("idx_ready")
        bm_ready = sem("bm_ready")
        w_t = sem("w_t")
        w_tc = sem("w_tc")
        w_c = sem("w_c")
        w_ready = sem("w_ready")

        sp_steps = sem("sp_steps")
        pool_steps = sem("pool_steps")
        staged = sem("staged")
        ends_ready = sem("ends_ready")
        ends_row = sem("ends_row")
        carry_row = sem("carry_row")
        carry_in = sem("carry_in")
        deg_ready = sem("deg_ready")
        deg_out = sem("deg_out")
        spilled = sems("spilled", RING)
        copied = sems("copied", 2)
        rest_copied = sem("rest_copied")

        class Round:
            def __init__(self, p, wide):
                self.wide = wide
                self.src_in = sems(f"src_in_{p}_", RING)
                self.dst_in = sems(f"dst_in_{p}_", RING)
                self.rows_in = sems(f"rows_in_{p}_", RING)
                self.turned = sem(f"turned_{p}")
                self.scan_a = sem(f"scan_a_{p}")
                self.scanned = sem(f"scanned_{p}")
                self.hT_ready = sem(f"hT_ready_{p}")
                self.gated = sem(f"gated_{p}")
                self.rz_ready = sem(f"rz_ready_{p}")
                self.rh_done = sem(f"rh_done_{p}")
                self.npre_done = sem(f"npre_done_{p}")
                self.tanh_done = sem(f"tanh_done_{p}")
                self.diff_done = sem(f"diff_done_{p}")
                self.zd_done = sem(f"zd_done_{p}")
                self.updated = sem(f"updated_{p}")

        R1, R2 = Round("1", RING), Round("2", WIDE)

        ln_in = sems("ln_in", 4)
        ln_out = sems("ln_out", 4)
        ln_bn = sem("ln_bn")
        ln_chain = sem("ln_chain")
        ln_coef = sem("ln_coef")
        ln_done = sem("ln_done")
        ln_done_v = sem("ln_done_v")

        h1_staged = sem("h1_staged")
        sct_staged = sem("sct_staged")
        scattered = sems("scattered", RING)

        staged2 = sem("staged2")
        a_hi_ready = sem("a_hi_ready")
        a_lo_ready = sem("a_lo_ready")
        xd_in = sems("xd_in", RING)
        y_done = sem("y_done")
        f_bn = sem("f_bn")
        f_sum = sem("f_sum")
        f_w = sem("f_w")
        f_sd = sem("f_sd")
        f_rs = sem("f_rs")
        f_coef = sem("f_coef")
        f_done = sem("f_done")
        out_staged = sem("out_staged")
        final_out = sems("final_out", WIDE)

        block = ctx.enter_context(nc.Block())

        def known(b):
            return isinstance(b, int)

        def at_least(b, n):
            return not known(b) or b >= n

        def body(step, wide, i):
            for u in range(wide):
                step(i * wide + u, u, i)

        def bodies(eng, step, wide, first, n, peel_last=True):
            body(step, wide, first)
            with eng.Fori(first + 1, first + n - (1 if peel_last else 0)) as i:
                body(step, wide, i)
            if peel_last:
                body(step, wide, first + n - 1)

        def round_1(eng, step_a, step_b):
            bodies(eng, step_a, RING, 0, HALF, False)
            bodies(eng, step_b, RING, HALF, BODIES1 - HALF)
            step_b(LAST, 0, BODIES1)

        def round_2(eng, step):
            bodies(eng, step, WIDE, 0, BODIES)
            step(LAST, 0, BODIES)

        def uses(R, u, i):
            return i * (R.wide // RING) + u // RING

        def stream(b, u, i, g):
            q = (b - FIRST_B) * 2 + g
            return q, (2 * u + g) % 4, (i - HALF) * 2 + u // 2

        def wait_apart(eng, semaphore, value):
            eng.wait_ge(semaphore, value)
            eng.sem_inc(sp_steps if eng.engine == mybir.EngineType.SP else pool_steps, 1)

        def cols(b):
            return bass.ds(b * SLOTS, SLOTS)

        def ln_rows(ap, s):
            if known(s) and s == LN_FULL:
                return ap[LN_FULL * P * LN_ROWS:N, :].rearrange("(p r) f -> p r f", r=LN_ROWS)
            return ap[bass.ds(s * (P * LN_ROWS), P * LN_ROWS), :].rearrange("(p r) f -> p r f", r=LN_ROWS)

        def ln_p(s):
            return LN_TAIL_P if known(s) and s == LN_FULL else P

        @block.sync
        def _(sp):
            def copy_chunk(n, g):
                sp.dma_start(h_table[bass.ds(n * COPY, COPY), :].rearrange("(a r) f -> a (r f)", a=16),
                             x[bass.ds(n * COPY, COPY), :].rearrange("(a r) f -> a (r f)", a=16))\
                  .then_inc(copied[g], 16)

            def copy_chunks(b):
                if known(b):
                    for n in range(PREP_CHUNKS + 3 * b, PREP_CHUNKS + 3 * b + 3):
                        wait_apart(sp, copied[n % 2], n // 2 * 16)
                        copy_chunk(n, n % 2)
                else:
                    for g in range(2):
                        wait_apart(sp, copied[g], b * 16 + (PREP_CHUNKS + RING) // 2 * 16)
                        copy_chunk(b * 2 + (PREP_CHUNKS + RING + g), g)

            sp.dma_start(dst_s[1:1 + E].rearrange("(a n) -> a n", a=8),
                         dst.rearrange("(a n) -> a n", a=8)).then_inc(lists_in, 16)
            sp.dma_start(src_s[0:E].rearrange("(a n) -> a n", a=8),
                         src.rearrange("(a n) -> a n", a=8)).then_inc(lists_in, 16)
            sp.wait_ge(pad_set, 2)
            sp.dma_start(dst_s[0:1].rearrange("(a n) -> a n", a=1), pad_idx[:, 0:1]).then_inc(lists_in, 16)
            sp.dma_start(dst_s[1 + E:EP + 2].rearrange("(a n) -> a n", a=1),
                         pad_idx[:, 0:EP + 1 - E]).then_inc(lists_in, 16)
            sp.dma_start(src_s[E:EP].rearrange("(a n) -> a n", a=1),
                         pad_idx[:, P:P + EP - E]).then_inc(lists_in, 16)
            sp.wait_ge(lists_in, 80)
            for k, (a, o) in enumerate(((dst_s, 1), (dst_s, 2), (src_s, 0), (dst_s, 0))):
                sp.dma_start(raw_idx[k][:, 0:P],
                             a[o:o + P * P].rearrange("(t p) -> t p", p=P)).then_inc(idx_in, 16)
                sp.dma_start(raw_idx[k][0:NT - P, P:2 * P],
                             a[o + P * P:o + NT * P].rearrange("(t p) -> t p", p=P)).then_inc(idx_in, 16)
            for t in range(2):
                sp.dma_start(wmsg_sb[t], W_msg[t].rearrange("(c m) f -> m c f", c=2)).then_inc(w_in, 16)
                sp.dma_start(wih_sb[t], W_ih[t].rearrange("(g m) f -> m g f", g=3)).then_inc(w_in, 16)
                sp.dma_start(whh_sb[t], W_hh[t].rearrange("(g m) f -> m g f", g=3)).then_inc(w_in, 16)
                for c in range(2):
                    sp.dma_start(bm_col[t][:, c:c + 1],
                                 b_msg[t, c * P:(c + 1) * P].rearrange("(p a) -> p a", a=1)).then_inc(w_in, 16)
                sp.dma_start(bih_rep[t][64:96, :],
                             b_ih[t].rearrange("(a n) -> a n", a=1).broadcast_to([32, 3 * P])).then_inc(w_in, 16)
                sp.dma_start(bhh_rep[t][64:96, :],
                             b_hh[t].rearrange("(a n) -> a n", a=1).broadcast_to([32, 3 * P])).then_inc(w_in, 16)

            copy_chunk(0, 0)
            sp.wait_ge(copied[0], 16)
            copy_chunk(1, 1)

            sp.wait_ge(deg_ready, 1)
            for k, t in enumerate((b_same, b_hi, b_lo)):
                sp.dma_start(rows_d[k, 0:P * P].rearrange("(t p) -> t p", p=P), t[:, 0:P]).then_inc(deg_out, 16)
                sp.dma_start(rows_d[k, P * P:EP].rearrange("(t p) -> t p", p=P),
                             t[0:NT - P, P:2 * P]).then_inc(deg_out, 16)
            sp.wait_ge(deg_out, 6 * 16)

            def deg_store():
                sp.dma_start(deg_d[0, 0:P * P].rearrange("(t p) -> t p", p=P), f_deg[:, 0:P]).then_inc(deg_out, 16)
                sp.dma_start(deg_d[0, P * P:EP].rearrange("(t p) -> t p", p=P),
                             f_deg[0:NT - P, P:2 * P]).then_inc(deg_out, 16)

            def rows_load(R, b, u):
                k = u % RING
                if at_least(b, RING):
                    sp.wait_ge(R.gated, 2 * (b - RING) + 2)
                sp.dma_start(same[k][:, :], rows_d[0:1, cols(b)].broadcast_to([P, SLOTS]))\
                  .then_inc(R.rows_in[k], 16)
                for r in (1, 2):
                    sp.dma_start(degl[k][32 * (r - 1):32 * (r - 1) + 3, :],
                                 rows_d[r:r + 1, cols(b)].broadcast_to([3, SLOTS])).then_inc(R.rows_in[k], 16)
                if R is R2:
                    sp.dma_start(deg_rep[k][:, :], deg_d[:, cols(b)].broadcast_to([P, SLOTS])).then_inc(R.rows_in[k], 16)

            def ln_load(s, k, before):
                if not known(before) or before > 0:
                    wait_apart(sp, ln_out[k], before * 16)
                sp.dma_start(lnbuf[k][0:ln_p(s)], ln_rows(x, s)).then_inc(ln_in[k], 16)

            def ln_store(s, k):
                sp.wait_ge(ln_done, s + 1)
                sp.wait_ge(ln_done_v, s + 1)
                sp.dma_start(ln_rows(out, s), lnbuf[k][0:ln_p(s)]).then_inc(ln_out[k], 16)

            def spill(b, u, i):
                sp.wait_ge(R1.dst_in[u % RING], (uses(R1, u, i) + 1) * 16 * TILES)
                sp.dma_start(xd_spill[bass.ds(b, 1)].rearrange("a p f -> (a p) f"),
                             dstbuf[u % RING][:, :]).then_inc(spilled[u % RING], 16)

            def step_a(b, u, i):
                rows_load(R1, b + 2, u + 2)
                spill(b, u, i)
                copy_chunks(b)

            def step_b(b, u, i):
                if not known(b) or b + 2 <= LAST:
                    rows_load(R1, b + 2, u + 2)
                spill(b, u, i)
                for g in range(2):
                    q, k, before = stream(b, u, i, g)
                    if at_least(b, FIRST_B + 1):
                        ln_store(q - 2, (k + 2) % 4)
                    if not known(q) or q + 2 <= LN_FULL:
                        ln_load(q + 2, (k + 2) % 4, before + (k >= 2))

            rows_load(R1, 0, 0)
            rows_load(R1, 1, 1)
            deg_store()
            sp.wait_ge(deg_out, 8 * 16)
            sp.dma_start(h_table[CHUNKS * COPY:N, :].rearrange("(a r) f -> a (r f)", a=16),
                         x[CHUNKS * COPY:N, :].rearrange("(a r) f -> a (r f)", a=16)).then_inc(rest_copied, 16)
            ln_load(0, 0, 0)
            ln_load(1, 1, 0)
            round_1(sp, step_a, step_b)

            sp.wait_ge(R1.updated, 2 * NB)
            for k in (1, 2):
                sp.wait_ge(ln_out[k], LN_FULL // 4 * 16)
            for u in range(RING):
                rows_load(R2, u, u)
            ln_store(LN_FULL, 0)
            for u in range(RING):
                sp.wait_ge(spilled[u], (BODIES1 + (u == 0)) * 16)
            sp.wait_ge(ln_out[3], LN_FULL // 4 * 16)

            def xd_load(b, u):
                k = u % RING
                if at_least(b, RING):
                    sp.wait_ge(y_done, 2 * (b - RING) + 2)
                sp.dma_start(xd[k][:, :, :],
                             xd_spill[bass.ds(b, 1)].rearrange("a p (t f) -> (a p) t f", t=TILES))\
                  .then_inc(xd_in[k], 16)

            def step_2(b, u, i):
                if at_least(b, RING):
                    rows_load(R2, b, u)
                xd_load(b, u)

            round_2(sp, step_2)

        @block.gpsimd
        def _(pool):
            nc.gpsimd.memset(pad_idx[:, 0:P], -1).then_inc(pad_set, 1)
            nc.gpsimd.memset(pad_idx[:, P:2 * P], 0).then_inc(pad_set, 1)
            nc.gpsimd.memset(ident[:, :], 0.0).then_inc(consts, 1)
            pool.wait_ge(consts, 1)
            nc.gpsimd.affine_select(out=ident[:, :], in_=ident[:, :], compare_op=ALU.not_equal, fill=1.0,
                                    base=0, pattern=[[-1, P]], channel_multiplier=1).then_inc(consts, 1)
            nc.gpsimd.memset(eps_col[:, :], EPS).then_inc(consts, 1)

            def gather(buf, table, idx, k, done):
                for t in range(TILES):
                    nc.gpsimd.indirect_dma_start(
                        out=buf[:, t * P:(t + 1) * P], out_offset=None, in_=table,
                        in_offset=bass.IndirectOffsetOnAxis(ap=idx[:, k * TILES + t:k * TILES + t + 1], axis=0),
                    ).then_inc(done, 16)

            def scatter(table, buf, idx, t0, done):
                for t in range(TILES):
                    nc.gpsimd.indirect_dma_start(
                        out=table, out_offset=bass.IndirectOffsetOnAxis(ap=idx[:, t:t + 1], axis=0),
                        in_=buf[:, (t0 + t) * P:(t0 + t + 1) * P], in_offset=None,
                        bounds_check=N - 1, oob_is_err=False,
                    ).then_inc(done, 16)

            def gather_src(b, u):
                wait_apart(pool, staged, b + 1)
                if at_least(b, RING):
                    wait_apart(pool, R1.turned, b - RING + 1)
                gather(srcbuf[u % RING], x, stage[u % RING], 0, R1.src_in[u % RING])

            def gather_dst(b, u, i):
                k = u % RING
                if at_least(b, RING):
                    wait_apart(pool, R1.updated, 2 * (b - RING) + 2)
                    wait_apart(pool, spilled[k], uses(R1, u, i) * 16)
                gather(dstbuf[k], x, stage[k], 1, R1.dst_in[k])

            def scatter_1(q, k):
                wait_apart(pool, sct_staged, q + 1)
                wait_apart(pool, h1_staged, q + 1)
                scatter(h_table, sctbuf[k], stage_out[k], 0, scattered[k])

            def step_a(b, u, i):
                gather_src(b, u)
                gather_dst(b, u, i)

            def step_b(b, u, i):
                gather_src(b, u)
                if known(b) and b == FIRST_B + SCT_LAG:
                    for g in range(2):
                        pool.wait_ge(copied[g], CHUNKS // 2 * 16)
                    pool.wait_ge(rest_copied, 16)
                q, k, _ = stream(b, u, i, 0)
                if at_least(b, FIRST_B + SCT_LAG):
                    scatter_1(q - 2 * SCT_LAG, (k - 2 * SCT_LAG) % 4)
                gather_dst(b, u, i)
                if at_least(b, FIRST_B + SCT_LAG):
                    scatter_1(q + 1 - 2 * SCT_LAG, (k + 1 - 2 * SCT_LAG) % 4)

            round_1(pool, step_a, step_b)
            for j in range(2 * (LAST - FIRST_B - SCT_LAG) + 2, NB):
                scatter_1(j, j % 4)
            for k in range(4):
                pool.wait_ge(scattered[k], (LAST // 4 + (k == 0)) * 16 * TILES)

            def gather_2(b, u):
                wait_apart(pool, staged2, b + 1)
                if at_least(b, RING):
                    wait_apart(pool, R2.turned, b - RING + 1)
                gather(srcbuf[u % RING], h_table, stage[u % RING], 0, R2.src_in[u % RING])

            def scatter_2(b, u):
                wait_apart(pool, out_staged, b + 1)
                wait_apart(pool, f_done, b + 1)
                scatter(out, y[u][:, :, :].rearrange("p r f -> p (r f)"), stage_out[u], 0, final_out[u])

            def step_2(b, u, i):
                gather_2(b, u)
                if known(b) and b == LAG:
                    for k in range(4):
                        pool.wait_ge(ln_out[k], (LN_FULL // 4 + (k == 0)) * 16)
                if at_least(b, LAG):
                    scatter_2(b - LAG, (u - LAG) % WIDE)

            round_2(pool, step_2)
            for b in range(LAST - LAG + 1, LAST + 1):
                scatter_2(b, b % WIDE)
            for u in range(WIDE):
                pool.wait_ge(final_out[u], (BODIES + (u == 0)) * 16 * TILES)

        @block.tensor
        def _(pe):
            pe.wait_ge(consts, 2)
            pe.wait_ge(idx_f, 1)
            for k, f in enumerate((f_idx[2], f_node, f_out)):
                for c in range(2):
                    last = nc.tensor.transpose(psG[k % 2][:, k // 2, c * P:(c + 1) * P], f[:, c * P:(c + 1) * P],
                                               ident[:, :])
            last.then_inc(idx_t, 1)
            pe.wait_ge(ends_ready, 1)
            pe.wait_ge(idx_ready, 1)
            for k, f in enumerate((f_local, f_head)):
                for c in range(2):
                    last = nc.tensor.matmul(psS[1][0:1, (2 * k + c) * P:(2 * k + c + 1) * P],
                                            f[:, c * P + P - 1:c * P + P], ident[:, :], start=True, stop=True)
            last.then_inc(ends_row, 1)

            def turn_weights(t):
                for c in range(2):
                    for o, g in enumerate((2, 0, 1)):
                        nc.tensor.transpose((psS if c == 0 else psD)[t][:, o * P:(o + 1) * P],
                                            wih_sb[t][:, g, c * P:(c + 1) * P], ident[:, :])
                for g in range(3):
                    last = nc.tensor.transpose(psG[t][:, 0, g * P:(g + 1) * P], whh_sb[t][:, g, :], ident[:, :])
                last.then_inc(w_t, 1)

            def fuse(t):
                pe.wait_ge(w_tc, t + 1)
                for c in range(2):
                    nc.tensor.matmul(psS[t][:, 0:3 * P], wmsg_sb[t][:, c, 0:P], wihT[t][:, c, :],
                                     start=(c == 0), stop=(c == 1))
                for c in range(2):
                    nc.tensor.matmul(psD[t][:, 0:3 * P], wmsg_sb[t][:, c, P:2 * P], wihT[t][:, c, :],
                                     start=(c == 0), stop=(c == 1))
                pe.wait_ge(bm_ready, 1)
                for c in range(2):
                    last = nc.tensor.matmul(psG[t][0:96, 1, 0:3 * P], bm_rep[t][:, c, :], wihT[t][:, c, :],
                                            start=(c == 0), stop=(c == 1))
                last.then_inc(w_c, 1)

            pe.wait_ge(w_in, 2 * 7 * 16)
            turn_weights(0)
            pe.wait_ge(carry_row, 1)
            for c in range(2):
                last = nc.tensor.matmul(psD[1][:, c:c + 1], carry[0:1, c * P:(c + 1) * P], ones_f[0:1, 0:1],
                                        start=True, stop=True)
            last.then_inc(carry_in, 1)
            fuse(0)
            pe.wait_ge(deg_ready, 1)
            turn_weights(1)
            fuse(1)
            pe.wait_ge(w_ready, 1)

            def turn(R, b, u, i, dst_n):
                k, v = u % RING, u % 2
                pe.wait_ge(R.src_in[k], (uses(R, u, i) + 1) * 16 * TILES)
                pe.wait_ge(R.dst_in[k], (uses(R, u, i) + 1) * dst_n)
                if at_least(b, 2):
                    pe.wait_ge(R.scanned, b - 1)
                for t in range(TILES):
                    nc.tensor.transpose(psS[v][:, t * P:(t + 1) * P], srcbuf[k][:, t * P:(t + 1) * P], ident[:, :])
                for t in range(TILES):
                    last = nc.tensor.transpose(psD[v][:, t * P:(t + 1) * P], dstbuf[k][:, t * P:(t + 1) * P],
                                               ident[:, :])
                last.then_inc(R.turned, 1)

            def gates(R, w, b, u, i, groups=(0, 1), split_h=True):
                v = u % 2
                pe.wait_ge(R.scanned, b + 1)
                pe.wait_ge(R.hT_ready, b + 1)
                if R is R2:
                    pe.wait_ge(a_hi_ready, b + 1)
                    pe.wait_ge(a_lo_ready, b + 1)
                pe.wait_ge(R.rows_in[u % RING], (uses(R, u, i) + 1) * (48 if R is R1 else 64))
                for g in groups:
                    q = 2 * b + g
                    if at_least(b, 1):
                        pe.wait_ge(R.npre_done, q - 1)
                    for t in range(2):
                        c = slice((2 * g + t) * P, (2 * g + t + 1) * P)
                        G = psG[g][:, t, :]
                        nc.tensor.matmul(G, degl[u % RING][:, c], WB[w][:, :], start=True, stop=False)
                        nc.tensor.matmul(G[:, 0:3 * P], dhT[v][:, c], WD[w][:, :], start=False, stop=False)
                        if R is R1:
                            nc.tensor.matmul(G[:, 0:3 * P], aT[v][:, c], WA[w][:, :], start=False, stop=False)
                        else:
                            nc.tensor.matmul(G[:, 0:3 * P], aT_hi[v][:, c], WA[w][:, :], start=False, stop=False)
                            nc.tensor.matmul(G[:, 0:3 * P], aT_hi[v][:, c], WA_lo[:, :], start=False, stop=False)
                            nc.tensor.matmul(G[:, 0:3 * P], aT_lo[v][:, c], WA[w][:, :], start=False, stop=False)
                        if split_h:
                            hi, lo = WH_parts[w]
                            nc.tensor.matmul(G[:, P:4 * P], hT_hi[v][:, c], hi[:, :], start=False, stop=False)
                            nc.tensor.matmul(G[:, P:4 * P], hT_hi[v][:, c], lo[:, :], start=False, stop=False)
                            last = nc.tensor.matmul(G[:, P:4 * P], hT_lo[v][:, c], hi[:, :], start=False, stop=True)
                        else:
                            last = nc.tensor.matmul(G[:, P:4 * P], hT[v][:, c], WH[w][:, :], start=False, stop=True)
                    last.then_inc(R.gated, 1)

            def turn_next(R, b, u, i, dst_n):
                if not known(b) or b < LAST:
                    turn(R, b + 1, (u + 1) % R.wide, i + (u == R.wide - 1), dst_n)

            def step_a(b, u, i):
                turn_next(R1, b, u, i, 16 * TILES)
                gates(R1, 0, b, u, i)

            def step_b(b, u, i):
                split_h = known(b) and b == FIRST_B
                gates(R1, 0, b, u, i, (0,), split_h)
                turn_next(R1, b, u, i, 16 * TILES)
                gates(R1, 0, b, u, i, (1,), split_h)

            turn(R1, 0, 0, 0, 16 * TILES)
            round_1(pe, step_a, step_b)

            def step_2(b, u, i):
                turn_next(R2, b, u, i, 1)
                gates(R2, 1, b, u, i)

            pe.wait_ge(w_ready, 2)
            turn(R2, 0, 0, 0, 1)
            round_2(pe, step_2)

        @block.scalar
        def _(act):
            for t in range(2):
                act.wait_ge(w_t, t + 1)
                nc.scalar.activation(wihT[t][:, 0, :], psS[t][:, 0:3 * P], ACT.Copy)
                nc.scalar.activation(wihT[t][:, 1, :], psD[t][:, 0:3 * P], ACT.Copy)
                if t == 0:
                    nc.scalar.activation(WH0_parts[0][:, :], psG[t][:, 0, 0:3 * P], ACT.Copy)
                nc.scalar.activation(WH[t][:, :], psG[t][:, 0, 0:3 * P], ACT.Copy).then_inc(w_tc, 1)

            def evac(R, b, u, split_h=True):
                act.wait_ge(R.turned, b + 1)
                if at_least(b, 2):
                    act.wait_ge(R.gated, 2 * (b - 1))
                to = (hT_hi if split_h else hT)[u % 2]
                nc.scalar.activation(to[:, :], psD[u % 2][:, :], ACT.Copy).then_inc(R.hT_ready, 1)

            def a_high(b, u):
                act.wait_ge(R2.scan_a, b + 1)
                nc.scalar.activation(aT_hi[u % 2][:, :], aT[u % 2][:, :], ACT.Copy).then_inc(a_hi_ready, 1)

            def sigmoids(R, b, g):
                q = 2 * b + g
                act.wait_ge(R.gated, q + 1)
                if at_least(b, 1):
                    act.wait_ge(R.zd_done, q - 1)
                nc.scalar.activation(rz[g][:, :, :], psG[g][:, :, P:3 * P], ACT.Sigmoid).then_inc(R.rz_ready, 1)

            def tanhs(R, b, g):
                act.wait_ge(R.npre_done, 2 * b + g + 1)
                nc.scalar.activation(nn[g][:, :, :], npre[g][:, :, :], ACT.Tanh).then_inc(R.tanh_done, 1)

            def ln_apply(s, k, rows):
                act.wait_ge(ln_coef, s + 1)
                n, v = ln_p(s), k % 2
                for r in rows:
                    last = nc.scalar.activation(lnbuf[k][0:n, r, :], lnbuf[k][0:n, r, :], ACT.Identity,
                                                bias=small[v][0:n, 7, r:r + 1], scale=small[v][0:n, 6, r:r + 1])
                last.then_inc(ln_done, 1)

            def stage_h1(q, k, before):
                act.wait_ge(R1.updated, 2 * q + 2)
                if known(q) and q == 0:
                    act.wait_ge(R1.gated, 2 * FIRST_B + 2)
                if at_least(q, 4):
                    act.wait_ge(scattered[k], before * 16 * TILES)
                nc.scalar.activation(sctbuf[k][:, :], h1[:, cols(q)], ACT.Copy).then_inc(h1_staged, 1)

            def step_a(b, u, i):
                if at_least(b, 1):
                    tanhs(R1, b - 1, 1)
                evac(R1, b + 1, u + 1)
                sigmoids(R1, b, 0)
                tanhs(R1, b, 0)
                sigmoids(R1, b, 1)

            def step_b(b, u, i):
                for g in range(2):
                    q, k, before = stream(b, u, i, g)
                    if g == 0:
                        tanhs(R1, b - 1, 1)
                    else:
                        tanhs(R1, b, 0)
                        if not known(b) or b < LAST:
                            evac(R1, b + 1, u + 1, False)
                    sigmoids(R1, b, g)
                    if not known(q) or q <= PAIRS_UP_TO:
                        stage_h1(q, k, before)
                    elif g == 1:
                        stage_h1(b - 1, (b - 1) % 4, (b - 1) // 4)
                    if at_least(q, 1) and (not known(q) or q < LN_FULL):
                        ln_apply(q - 1, (k - 1) % 4, range(ACT_ROWS))

            evac(R1, 0, 0)
            round_1(act, step_a, step_b)
            tanhs(R1, LAST, 1)
            stage_h1(LAST, 0, LAST // 4)

            def load_h(b, u):
                if at_least(b, RING):
                    act.wait_ge(R2.updated, 2 * (b - RING) + 2)
                nc.scalar.activation(dstbuf[u % RING][:, :], h1[:, cols(b)], ACT.Copy)\
                  .then_inc(R2.dst_in[u % RING], 1)

            def f_sqrt(b, v):
                act.wait_ge(f_w, b + 1)
                nc.scalar.activation(small[v][:, 4, 0:TILES], small[v][:, 3, 0:TILES], ACT.Sqrt,
                                     bias=eps_col[:, :], scale=0.25).then_inc(f_sd, 1)

            def f_apply(b, u, tiles):
                act.wait_ge(f_coef, b + 1)
                v = u % 2
                for t in tiles:
                    last = nc.scalar.activation(y[u][:, t, :], y[u][:, t, :], ACT.Identity,
                                                bias=small[v][:, 7, t:t + 1], scale=small[v][:, 5, t:t + 1])
                if tiles[-1] == TILES - 1:
                    last.then_inc(f_done, 1)

            for u in range(RING):
                act.wait_ge(spilled[u], (BODIES1 + (u == 0)) * 16)
            for u in range(RING):
                load_h(u, u)
            for s in (LN_FULL - 1, LN_FULL):
                ln_apply(s, s % 4, range(ACT_ROWS))
            act.wait_ge(R1.gated, 2 * NB)
            evac(R2, 0, 0)
            for k in range(4):
                act.wait_ge(scattered[k], (LAST // 4 + (k == 0)) * 16 * TILES)
            a_high(0, 0)

            def step_2(b, u, i):
                if not known(b) or b < LAST:
                    evac(R2, b + 1, u + 1)
                if at_least(b, 1):
                    tanhs(R2, b - 1, 1)
                sigmoids(R2, b, 0)
                if at_least(b, 3):
                    f_apply(b - 3, (u - 3) % WIDE, (2, 3))
                if not known(b) or b < LAST:
                    a_high(b + 1, u + 1)
                if at_least(b, 2):
                    f_sqrt(b - 2, (u - 2) % 2)
                sigmoids(R2, b, 1)
                tanhs(R2, b, 0)
                if not known(b) or b + RING - 1 <= LAST and b >= 1:
                    load_h(b + RING - 1, u + RING - 1)
                if at_least(b, 2):
                    f_apply(b - 2, (u - 2) % WIDE, (0, 1))

            round_2(act, step_2)
            tanhs(R2, LAST, 1)
            f_apply(LAST - 2, (LAST - 2) % WIDE, (2, 3))
            for b in (LAST - 1, LAST):
                f_sqrt(b, b % 2)
                f_apply(b, b % WIDE, range(TILES))

        @block.vector
        def _(dve):
            links = [0]

            def link(ins):
                links[0] += 1
                ins.then_inc(prep_v, 1)
                dve.wait_ge(prep_v, links[0])

            for k in range(RING):
                nc.vector.memset(degl[k][0:64, :], 0.0)
                nc.vector.memset(degl[k][64:96, :], 1.0)
            last = nc.vector.memset(ones_f, 1.0)
            for k in range(2):
                nc.vector.memset(aT[k][:, SLOTS - 1:SLOTS], 0.0)
                nc.vector.memset(dhT[k][:, SLOTS - 1:SLOTS], 0.0)
            nc.vector.memset(carry[0:1, 0:1], 0.0)
            for k in range(4):
                nc.vector.memset(f_idx[k], 0.0)
            nc.vector.memset(f_same, 0.0)
            link(nc.vector.memset(f_out, 0.0))
            dve.wait_ge(idx_in, 8 * 16)
            for k in range(4):
                nc.vector.tensor_copy(f_idx[k][:, 0:P], raw_idx[k][:, 0:P])
                last = nc.vector.tensor_copy(f_idx[k][0:NT - P, P:2 * P], raw_idx[k][0:NT - P, P:2 * P])
            link(last)
            link(nc.vector.tensor_tensor(f_same, f_idx[0], f_idx[1], ALU.is_equal))
            nc.vector.tensor_tensor(f_prev, f_idx[0], f_idx[3], ALU.is_equal)
            for c in range(2):
                h = slice(c * P, (c + 1) * P)
                nc.vector.tensor_scalar(f_head[:, h], f_idx[0][:, h], f_idx[3][:, c * P:c * P + 1], None,
                                        ALU.is_equal)
            link(nc.vector.tensor_scalar(f_node, f_idx[0], 0.0, None, ALU.max))
            nc.vector.scalar_tensor_tensor(out=f_out, in0=f_same, scalar=SKIP, in1=f_node,
                                           op0=ALU.mult, op1=ALU.add).then_inc(idx_f, 1)
            dve.wait_ge(idx_t, 1)
            for k in range(3):
                last = nc.vector.tensor_copy(
                    idx_all[:, :, k, :], psG[k % 2][:, k // 2, 0:NT].rearrange("p (b t) -> p b t", t=TILES))
            link(last)

            def stage_idx(b, u, ready, scat=False):
                d, a = (stage_out, slice(2, 3)) if scat else (stage, slice(0, 2))
                nc.vector.tensor_copy(d[u][:, :].rearrange("p (b k t) -> p b k t", b=1, t=TILES),
                                      idx_all[:, bass.ds(b, 1), a, :]).then_inc(ready, 1)

            for u in range(RING):
                stage_idx(u, u, staged)
            for c in range(2):
                h = slice(c * P, (c + 1) * P)
                last = nc.vector.tensor_tensor_scan(f_local[:, h], f_prev[:, h], ones_f[:, h], 0.0,
                                                    ALU.mult, ALU.add)
            last.then_inc(ends_ready, 1)
            dve.wait_ge(consts, 3)
            link(nc.vector.tensor_tensor(sel[:, :], ident[:, 0:3], ident[:, 32:35], ALU.add))
            nc.vector.tensor_tensor(sel[:, :], sel[:, :], ident[:, 64:67], ALU.add).then_inc(idx_ready, 1)

            dve.wait_ge(ends_row, 1)
            link(nc.vector.tensor_copy(ends[0:1, :], psS[1][0:1, :]))
            nc.vector.tensor_tensor_scan(carry[0:1, 1:2 * P + 1], ends[0:1, 2 * P:4 * P], ends[0:1, 0:2 * P], 0.0,
                                         ALU.mult, ALU.add).then_inc(carry_row, 1)
            dve.wait_ge(carry_in, 1)
            link(nc.vector.tensor_copy(carry_col, psD[1][:, 0:2]))
            for c in range(2):
                h = slice(c * P, (c + 1) * P)
                last = nc.vector.scalar_tensor_tensor(out=f_deg[:, h], in0=f_head[:, h], scalar=carry_col[:, c:c + 1],
                                                      in1=f_local[:, h], op0=ALU.mult, op1=ALU.add)
            link(last)
            nc.vector.tensor_copy(b_same, f_prev)
            link(nc.vector.tensor_copy(b_hi, f_deg))
            nc.vector.tensor_tensor(b_lo, f_deg, b_hi, ALU.subtract).then_inc(deg_ready, 1)

            dve.wait_ge(w_in, 2 * 7 * 16)
            for t in range(2):
                for c in range(2):
                    last = nc.vector.tensor_copy(bm_rep[t][:, c, :], bm_col[t][:, c:c + 1].broadcast_to([P, 96]))
            last.then_inc(bm_ready, 1)

            def take_products(t):
                dve.wait_ge(w_c, t + 1)
                hi, lo = WH_parts[t]
                last = nc.vector.tensor_copy(WA[t][:, :], psS[t][:, 0:3 * P])
                nc.vector.tensor_tensor(lo[:, :], psG[t][:, 0, 0:3 * P], hi[:, :].bitcast(F32), ALU.subtract)
                if t == 1:
                    link(last)
                    nc.vector.tensor_tensor(WA_lo[:, :], psS[t][:, 0:3 * P], WA[t][:, :].bitcast(F32), ALU.subtract)
                nc.vector.tensor_copy(WD[t][:, :], psD[t][:, 0:3 * P])
                return nc.vector.tensor_copy(bias_f[t][0:64, 0:3 * P], psG[t][0:64, 1, 0:3 * P])

            def bias_rows(t):
                B, bi, bh = bias_f[t], bih_rep[t], bhh_rep[t]
                nc.vector.memset(B[0:64, 3 * P:4 * P], 0.0)
                nc.vector.tensor_copy(B[64:96, 0:P], bi[64:96, 2 * P:3 * P])
                nc.vector.tensor_tensor(B[64:96, P:3 * P], bi[64:96, 0:2 * P], bh[64:96, 0:2 * P], ALU.add)
                link(nc.vector.tensor_copy(B[64:96, 3 * P:4 * P], bh[64:96, 2 * P:3 * P]))
                rem = B
                for k in range(3):
                    link(nc.vector.tensor_copy(part[t][k][0:96, :], rem[0:96, :]))
                    if k < 2:
                        link(nc.vector.tensor_tensor(rest[t][k][0:96, :], rem[0:96, :], part[t][k][0:96, :],
                                                     ALU.subtract))
                        rem = rest[t][k]
                link(nc.vector.tensor_scalar(pick[t][0][0:96, :], part[t][0][0:96, :], sel[0:96, 0:1], None, ALU.mult))
                link(nc.vector.scalar_tensor_tensor(out=pick[t][1][0:96, :], in0=part[t][1][0:96, :],
                                                    scalar=sel[0:96, 1:2], in1=pick[t][0][0:96, :],
                                                    op0=ALU.mult, op1=ALU.add))
                return nc.vector.scalar_tensor_tensor(out=WB[t][:, :], in0=part[t][2][0:96, :],
                                                      scalar=sel[0:96, 2:3], in1=pick[t][1][0:96, :],
                                                      op0=ALU.mult, op1=ALU.add)

            take_products(0)
            bias_rows(0)
            take_products(1).then_inc(w_ready, 1)

            def scan_src(R, b, u, i):
                v = u % 2
                dve.wait_ge(R.rows_in[u % RING], (uses(R, u, i) + 1) * (48 if R is R1 else 64))
                dve.wait_ge(R.turned, b + 1)
                if at_least(b, 2):
                    dve.wait_ge(R.gated, 2 * (b - 1))
                if at_least(b, 1):
                    dve.wait_ge(R.scan_a, b)
                nc.vector.tensor_tensor_scan(aT[v][:, :], same[u % RING][:, :], psS[v][:, :],
                                             aT[1 - v][:, SLOTS - 1:SLOTS], ALU.mult, ALU.add).then_inc(R.scan_a, 1)

            def scan_dst(R, b, u):
                v = u % 2
                dve.wait_ge(R.hT_ready, b + 1)
                if R is R1:
                    if at_least(b, 1):
                        dve.wait_ge(R.scanned, b)
                    nc.vector.tensor_tensor_scan(dhT[v][:, :], same[u % RING][:, :], psD[v][:, :],
                                                 dhT[1 - v][:, SLOTS - 1:SLOTS], ALU.mult, ALU.add)\
                      .then_inc(R.scanned, 1)
                else:
                    nc.vector.tensor_tensor(dhT[v][:, :], deg_rep[u % RING][:, :], psD[v][:, :], ALU.mult)\
                      .then_inc(R.scanned, 1)

            def h_low(R, b, u):
                v = u % 2
                dve.wait_ge(R.hT_ready, b + 1)
                nc.vector.tensor_tensor(hT_lo[v][:, :], psD[v][:, :], hT_hi[v][:, :].bitcast(F32),
                                        ALU.subtract)

            def a_low(b, u):
                v = u % 2
                dve.wait_ge(a_hi_ready, b + 1)
                nc.vector.tensor_tensor(aT_lo[v][:, :], aT[v][:, :], aT_hi[v][:, :].bitcast(F32), ALU.subtract)\
                  .then_inc(a_lo_ready, 1)

            def gate_hn(R, b, g):
                dve.wait_ge(R.rz_ready, 2 * b + g + 1)
                nc.vector.tensor_tensor(npre[g][:, :, :], rz[g][:, :, 0:P], psG[g][:, :, 3 * P:4 * P],
                                        ALU.mult).then_inc(R.rh_done, 1)

            def add_inn(R, b, g):
                dve.wait_ge(R.rh_done, 2 * b + g + 1)
                nc.vector.tensor_tensor(npre[g][:, :, :], npre[g][:, :, :], psG[g][:, :, 0:P],
                                        ALU.add).then_inc(R.npre_done, 1)

            def candidate(R, b, g):
                gate_hn(R, b, g)
                add_inn(R, b, g)

            def h_minus_n(R, b, u, g):
                h = dstbuf[u % RING][:, g * 2 * P:(g + 1) * 2 * P].rearrange("p (t f) -> p t f", t=2)
                dve.wait_ge(R.tanh_done, 2 * b + g + 1)
                nc.vector.tensor_tensor(dd[g][:, :, :], h, nn[g][:, :, :], ALU.subtract).then_inc(R.diff_done, 1)

            def times_z(R, b, g):
                dve.wait_ge(R.diff_done, 2 * b + g + 1)
                nc.vector.tensor_tensor(dd[g][:, :, :], rz[g][:, :, P:2 * P], dd[g][:, :, :], ALU.mult)\
                  .then_inc(R.zd_done, 1)

            def plus_n(R, b, g, to):
                dve.wait_ge(R.zd_done, 2 * b + g + 1)
                nc.vector.tensor_tensor(to, nn[g][:, :, :], dd[g][:, :, :], ALU.add).then_inc(R.updated, 1)

            def update(R, b, u, g, to, between=None):
                h_minus_n(R, b, u, g)
                if between:
                    between()
                times_z(R, b, g)
                plus_n(R, b, g, to)

            def h1_group(b, g):
                return h1[:, bass.ds(b * SLOTS + g * 2 * P, 2 * P)].rearrange("p (t f) -> p t f", t=2)

            def ln_chain_step(s, k, c):
                n, S, T = ln_p(s), small[k % 2], st[k % 2]
                row = [S[0:n, j, :] for j in range(8)]
                if c == 0:
                    dve.wait_ge(ln_bn, s + 1)
                    if at_least(s, 2):
                        dve.wait_ge(ln_done, s - 1)
                    nc.vector.tensor_tensor(row[0], T[0:n, :, 1], T[0:n, :, 4], ALU.add)
                    nc.vector.tensor_tensor(row[1], T[0:n, :, 1], T[0:n, :, 4], ALU.subtract)
                    last = nc.vector.tensor_tensor(row[2], T[0:n, :, 2], T[0:n, :, 5], ALU.add)
                else:
                    dve.wait_ge(ln_chain, s * (LN_STEPS - 1) + c)
                    if c == 1:
                        nc.vector.scalar_tensor_tensor(out=row[1], in0=row[1], scalar=-0.5, in1=row[1],
                                                       op0=ALU.mult, op1=ALU.mult)
                        last = nc.vector.tensor_scalar(row[2], row[2], -2.0 / P, -EPS / 2, ALU.mult, ALU.add)
                    elif c == 2:
                        last = nc.vector.tensor_tensor(row[3], row[1], row[2], ALU.add)
                    elif c == 3:
                        last = nc.vector.tensor_scalar(row[4].bitcast(I32), row[3].bitcast(I32), -0.5, GUESS,
                                                       ALU.mult, ALU.add)
                    elif c == LN_STEPS - 1:
                        nc.vector.tensor_scalar(row[6], row[4], 2.0, None, ALU.mult)
                        last = nc.vector.scalar_tensor_tensor(out=row[7], in0=row[0], scalar=-1.0, in1=row[4],
                                                              op0=ALU.mult, op1=ALU.mult)
                    elif (c - 4) % 3 == 0:
                        last = nc.vector.tensor_tensor(row[1], row[4], row[4], ALU.mult)
                    elif (c - 4) % 3 == 1:
                        last = nc.vector.tensor_tensor(row[1], row[1], row[3], ALU.mult)
                    else:
                        last = nc.vector.scalar_tensor_tensor(out=row[4], in0=row[1], scalar=1.5, in1=row[4],
                                                              op0=ALU.add, op1=ALU.mult)
                last.then_inc(ln_coef if c == LN_STEPS - 1 else ln_chain, 1)

            def ln_apply(s, k):
                n, v = ln_p(s), k % 2
                dve.wait_ge(ln_coef, s + 1)
                for r in range(ACT_ROWS, LN_ROWS):
                    last = nc.vector.tensor_scalar(lnbuf[k][0:n, r, :], lnbuf[k][0:n, r, :],
                                                   small[v][0:n, 6, r:r + 1], small[v][0:n, 7, r:r + 1],
                                                   ALU.mult, ALU.add)
                last.then_inc(ln_done_v, 1)

            def ln_stats(s, k, before, rows):
                n = ln_p(s)
                if rows[0] == 0:
                    dve.wait_ge(ln_in[k], before * 16 + 16)
                for r in rows:
                    last = nc.vector.bn_stats(st[k % 2][0:n, r, :], lnbuf[k][0:n, r, :])
                    if r == LN_ROWS - 1:
                        last.then_inc(ln_bn, 1)
                    if at_least(s, 1) and r < LN_STEPS:
                        ln_chain_step(s - 1, (k - 1) % 4, r)

            def next_indices(b, u, i):
                dve.wait_ge(R1.src_in[u % RING], (uses(R1, u, i) + 1) * 16 * TILES)
                dve.wait_ge(R1.dst_in[u % RING], (uses(R1, u, i) + 1) * 16 * TILES)
                stage_idx(b + RING, u % RING, staged)

            def sct_indices(q, k, before):
                if at_least(q, 4):
                    dve.wait_ge(scattered[k], before * 16 * TILES)
                stage_idx(q, k, sct_staged, scat=True)

            def step_a(b, u, i):
                next_indices(b, u, i)
                scan_src(R1, b + 1, (u + 1) % RING, i + (u == RING - 1))
                if at_least(b, 1):
                    update(R1, b - 1, u - 1, 1, h1_group(b - 1, 1))
                h_low(R1, b + 1, u + 1)
                candidate(R1, b, 0)
                scan_dst(R1, b + 1, u + 1)
                update(R1, b, u, 0, h1_group(b, 0))
                candidate(R1, b, 1)

            def step_b(b, u, i):
                more = not known(b) or b < LAST
                if not known(b) or b + RING <= LAST:
                    next_indices(b, u, i)
                for g in range(2):
                    q, k, before = stream(b, u, i, g)
                    if not known(q) or q <= PAIRS_UP_TO:
                        sct_indices(q, k, before)
                    elif g == 1:
                        sct_indices(b - 1, (b - 1) % 4, (b - 1) // 4)
                    streams = not known(q) or q < LN_FULL
                    if streams:
                        ln_stats(q, k, before, range(LN_STEPS))
                    if more and g == 1:
                        scan_src(R1, b + 1, (u + 1) % RING, i + (u == RING - 1))
                        scan_dst(R1, b + 1, u + 1)
                    tail = (lambda: ln_stats(q, k, before, range(LN_STEPS, LN_ROWS))) if streams else None
                    if g == 0:
                        update(R1, b - 1, u - 1, 1, h1_group(b - 1, 1), tail)
                    else:
                        update(R1, b, u, 0, h1_group(b, 0), tail)
                    candidate(R1, b, g)
                    if streams and at_least(q, 1):
                        ln_apply(q - 1, (k - 1) % 4)

            dve.wait_ge(w_ready, 1)
            scan_src(R1, 0, 0, 0)
            h_low(R1, 0, 0)
            scan_dst(R1, 0, 0)
            bias_rows(1).then_inc(w_ready, 1)
            round_1(dve, step_a, step_b)
            update(R1, LAST, 0, 1, h1_group(LAST, 1))
            sct_indices(LAST, 0, LAST // 4)
            for u in range(RING):
                stage_idx(u, u, staged2)
            ln_stats(LN_FULL, 0, LN_FULL // 4, range(LN_ROWS))
            ln_apply(LN_FULL - 1, (LN_FULL - 1) % 4)
            for c in range(LN_STEPS):
                ln_chain_step(LN_FULL, 0, c)
            ln_apply(LN_FULL, 0)

            dve.wait_ge(R1.scanned, NB)
            for k in range(2):
                last = nc.vector.memset(aT[k][:, SLOTS - 1:SLOTS], 0.0)
            link(last)
            for u in range(RING):
                dve.wait_ge(scattered[u], (LAST // 4 + (u == 0)) * 16 * TILES)
            dve.wait_ge(ln_out[1], LN_FULL // 4 * 16)

            def residual(b, u, i, g):
                k = u % RING
                if known(b) and b == 0 and g == 0:
                    for j in (0, 3):
                        dve.wait_ge(ln_out[j], (LN_FULL // 4 + (j == 0)) * 16)
                if g == 0:
                    dve.wait_ge(xd_in[k], uses(R2, u, i) * 16 + 16)
                    if not known(i) or i > 0:
                        dve.wait_ge(final_out[u], i * 16 * TILES)
                dve.wait_ge(R2.updated, 2 * b + g + 1)
                nc.vector.tensor_tensor(y[u][:, 2 * g:2 * g + 2, :], hout[g][:, :, :], xd[k][:, 2 * g:2 * g + 2, :],
                                        ALU.add)\
                  .then_inc(y_done, 1)

            def y_stats(b, u, g):
                dve.wait_ge(y_done, 2 * b + g + 1)
                for t in (2 * g, 2 * g + 1):
                    last = nc.vector.bn_stats(st[u % 2][:, t, :], y[u][:, t, :])
                if g == 1:
                    last.then_inc(f_bn, 1)

            def moments_1(b, v):
                S, T = small[v][:, :, 0:TILES], st[v][:, 0:TILES, :]
                dve.wait_ge(f_bn, b + 1)
                if at_least(b, 2):
                    dve.wait_ge(f_done, b - 1)
                nc.vector.tensor_tensor(S[:, 0, :], T[:, :, 1], T[:, :, 4], ALU.add)
                nc.vector.tensor_tensor(S[:, 1, :], T[:, :, 1], T[:, :, 4], ALU.subtract)
                nc.vector.tensor_tensor(S[:, 2, :], T[:, :, 2], T[:, :, 5], ALU.add).then_inc(f_sum, 1)

            def moments_2(b, v):
                S = small[v][:, :, 0:TILES]
                dve.wait_ge(f_sum, 2 * b + 1)
                nc.vector.tensor_tensor(S[:, 1, :], S[:, 1, :], S[:, 1, :], ALU.mult).then_inc(f_sum, 1)

            def moments_3(b, v):
                S = small[v][:, :, 0:TILES]
                dve.wait_ge(f_sum, 2 * b + 2)
                nc.vector.scalar_tensor_tensor(out=S[:, 3, :], in0=S[:, 2, :], scalar=4.0 / P, in1=S[:, 1, :],
                                               op0=ALU.mult, op1=ALU.add).then_inc(f_w, 1)

            def finish_1(b, v):
                dve.wait_ge(f_sd, b + 1)
                nc.vector.reciprocal(small[v][:, 5, 0:TILES], small[v][:, 4, 0:TILES]).then_inc(f_rs, 1)

            def finish_2(b, v):
                S = small[v][:, :, 0:TILES]
                dve.wait_ge(f_rs, b + 1)
                nc.vector.scalar_tensor_tensor(out=S[:, 7, :], in0=S[:, 0, :], scalar=-0.5, in1=S[:, 5, :],
                                               op0=ALU.mult, op1=ALU.mult).then_inc(f_coef, 1)

            def step_2(b, u, i):
                more = not known(b) or b < LAST
                prev = at_least(b, 1)
                pu, pi = (u - 1) % WIDE, i - (u == 0)
                if not known(b) or b + RING <= LAST:
                    dve.wait_ge(R2.src_in[u % RING], (uses(R2, u, i) + 1) * 16 * TILES)
                    stage_idx(b + RING, u % RING, staged2)
                if not known(i) or i > 0:
                    dve.wait_ge(final_out[u], i * 16 * TILES)
                stage_idx(b, u, out_staged, scat=True)
                if more:
                    scan_src(R2, b + 1, u + 1 if u + 1 < WIDE else 0, i + (u + 1 == WIDE))
                if prev:
                    h_minus_n(R2, b - 1, pu, 1)
                gate_hn(R2, b, 0)
                if prev:
                    times_z(R2, b - 1, 1)
                if more:
                    h_low(R2, b + 1, u + 1)
                add_inn(R2, b, 0)
                if more:
                    scan_dst(R2, b + 1, u + 1)
                if prev:
                    plus_n(R2, b - 1, 1, hout[1][:, :, :])
                if more:
                    a_low(b + 1, u + 1)
                if prev:
                    residual(b - 1, pu, pi, 1)
                if at_least(b, 2):
                    finish_1(b - 2, u % 2)
                if prev:
                    y_stats(b - 1, pu, 1)
                gate_hn(R2, b, 1)
                if at_least(b, 2):
                    finish_2(b - 2, u % 2)
                h_minus_n(R2, b, u, 0)
                add_inn(R2, b, 1)
                if prev:
                    moments_1(b - 1, pu % 2)
                times_z(R2, b, 0)
                if prev:
                    moments_2(b - 1, pu % 2)
                plus_n(R2, b, 0, hout[0][:, :, :])
                if prev:
                    moments_3(b - 1, pu % 2)
                residual(b, u, i, 0)
                y_stats(b, u, 0)

            scan_src(R2, 0, 0, 0)
            h_low(R2, 0, 0)
            scan_dst(R2, 0, 0)
            a_low(0, 0)
            round_2(dve, step_2)
            update(R2, LAST, 0, 1, hout[1][:, :, :])
            residual(LAST, 0, BODIES, 1)
            y_stats(LAST, 0, 1)
            moments_1(LAST, 0)
            moments_2(LAST, 0)
            moments_3(LAST, 0)
            for b in (LAST - 1, LAST):
                finish_1(b, b % 2)
                finish_2(b, b % 2)


_INS = ["x", "src", "dst", "L0_gnn_W_msg", "L0_gnn_b_msg", "L0_gnn_W_ih", "L0_gnn_W_hh", "L0_gnn_b_ih", "L0_gnn_b_hh"]


def kernel(**inputs):
    import numpy as np
    import concourse.bacc as bacc
    from concourse import mybir as mb
    from concourse.bass_utils import run_bass_kernel_spmd as run

    nc = bacc.Bacc("TRN2", target_bir_lowering=False, num_devices=1)
    arrays, args = {}, []
    for name in _INS:
        a = np.ascontiguousarray(inputs[name])
        arrays[f"in_{name}"] = a
        args.append(nc.dram_tensor(f"in_{name}", a.shape, mb.dt.from_np(a.dtype), kind="ExternalInput").ap())
    out = nc.dram_tensor("out_rows", arrays["in_x"].shape, mb.dt.float32, kind="ExternalOutput").ap()
    build(nc, *args, out)
    r = run(nc, [arrays], core_ids=[0])
    return r.results[0]["out_rows"]
```
